# Optimizing a Trainium2 kernel written in Bass

```python
import numpy as np
import jax
import jax.numpy as jnp

def _softmax(x, axis=-1):
    return jax.nn.softmax(x, axis=axis)

def _gelu(x):
    return jax.nn.gelu(x, approximate=True)

def _silu(x):
    return jax.nn.silu(x)

def _sigmoid(x):
    return jax.nn.sigmoid(x)

def _layernorm(x, axis=-1, eps=1e-05):
    m = jnp.mean(x, axis=axis, keepdims=True)
    v = jnp.var(x, axis=axis, keepdims=True)
    return (x - m) / jnp.sqrt(v + eps)

def _scatter_add(tgt, idx, src, axis=0):
    return tgt.at[idx].add(src)

def _segment_sum(src, seg, n):
    return jax.ops.segment_sum(src, seg, n)
kernel_name = 'mk_adaln_ffn_d1_seqx_r8_727acf'

def setup_inputs(seed: int=0):
    np.random.seed(seed)
    _w = jnp.asarray

    def _rec_inputs():
        import jax
        import jax.numpy as jnp
        _rk = jax.random.key(seed)
        x = -0.0003929 + 0.9999 * jax.random.normal(jax.random.fold_in(_rk, 1), (128, 32, 128), jnp.float32)
        _lenS = 32 - jax.random.randint(jax.random.fold_in(_rk, 7), (128,), 0, max(1, 32 // 4) + 1, jnp.int32)
        _lenS2 = 32 - jax.random.randint(jax.random.fold_in(_rk, 8), (128,), 0, max(1, 32 // 4) + 1, jnp.int32)
        cond_2048 = 0.00782532 + 1.00527 * jax.random.normal(jax.random.fold_in(_rk, 11), (128, 256), jnp.float32)
        return (x, cond_2048)
    x, cond_2048 = _rec_inputs()

    def _L0_cond_setup():
        import jax, jax.numpy as jnp
        import numpy as np
        B, S, D_MODEL, D_INNER, D_STATE = (4, 512, 128, 256, 16)
        key = jax.random.key(seed)
        ks = jax.random.split(key, 12)
        inp = {'x': jax.random.normal(ks[0], (B, S, D_MODEL), jnp.float32), 't_emb': jax.random.normal(ks[1], (B, D_INNER), jnp.float32), 'W_in': jax.random.normal(ks[2], (2 * D_INNER, D_MODEL), jnp.float32) * 0.02, 'W_conv': jax.random.normal(ks[3], (D_INNER, 1, 4), jnp.float32) * 0.1, 'b_conv': jnp.zeros((D_INNER,), jnp.float32), 'ln_g': jnp.ones((D_INNER,), jnp.float32), 'ln_b': jnp.zeros((D_INNER,), jnp.float32), 'W_xproj': jax.random.normal(ks[4], (3 * D_STATE, D_INNER), jnp.float32) * 0.02, 'W_dt': jax.random.normal(ks[5], (D_STATE, D_STATE), jnp.float32) * 0.01, 'b_dt': jax.random.uniform(ks[6], (D_STATE,), jnp.float32) * 0.1, 'A_log': jax.random.normal(ks[7], (D_STATE,), jnp.float32) * 0.1, 'D': jnp.ones((D_INNER,), jnp.float32) * 0.1, 'W_out': jax.random.normal(ks[8], (D_MODEL, D_INNER), jnp.float32) * 0.02}
        return inp
    _L0_cond_all = _L0_cond_setup()
    _L0_cond_in = {k: v for k, v in _L0_cond_all.items() if k in ('W_in', 'W_conv', 'b_conv', 'ln_g', 'ln_b', 'W_xproj', 'W_dt', 'b_dt', 'A_log', 'D', 'W_out')}
    del _L0_cond_all

    def _L0_ffn_setup():
        import jax, jax.numpy as jnp
        import numpy as np
        DIM = 128
        DEPTH = 6
        HEADS = 16
        DIM_HEAD = 64
        WINDOW = 32
        INNER = HEADS * DIM_HEAD
        DIM_INNER = int(DIM * 4 * 2 / 3)
        QK_SCALE = 8.0

        def shift_tokens(t):
            a, s = jnp.split(t, 2, -1)
            s = jnp.pad(s, ((0, 0), (1, 0), (0, 0)))[:, :-1]
            return jnp.concatenate([a, s], -1)

        def l2norm(t):
            return t / jnp.maximum(jnp.linalg.norm(t, axis=-1, keepdims=True), 1e-12)

        def rotate_half(x):
            x1, x2 = jnp.split(x, 2, -1)
            return jnp.concatenate([-x2, x1], -1)

        def rotary_tables(n):
            half = jnp.arange(0, DIM_HEAD, 2, dtype=jnp.float32)
            inv_freq = 1.0 / 10000.0 ** (half / DIM_HEAD)
            t = jnp.arange(n, dtype=jnp.float32)
            freqs = t[:, None] * inv_freq[None, :]
            freqs = jnp.concatenate([freqs, freqs], -1)
            base_scale = (half + 0.4 * DIM_HEAD) / (1.4 * DIM_HEAD)
            power = (t - n // 2) / (WINDOW // 2)
            scale = base_scale[None, :] ** power[:, None]
            scale = jnp.concatenate([scale, scale], -1)
            return (freqs, scale)

        def local_attention(q, k, v):
            b, h, n, d = q.shape
            w = WINDOW
            nw = n // w
            bq = q.reshape(b, h, nw, w, d)
            bk = k.reshape(b, h, nw, w, d)
            bv = v.reshape(b, h, nw, w, d)

            def look(t):
                p = jnp.pad(t, ((0, 0), (0, 0), (1, 0), (0, 0), (0, 0)))
                return jnp.concatenate([p[:, :, :nw], p[:, :, 1:]], axis=3)
            bk2, bv2 = (look(bk), look(bv))
            seq = jnp.arange(n).reshape(nw, w)
            seq_p = jnp.pad(seq, ((1, 0), (0, 0)), constant_values=-1)
            jt = jnp.concatenate([seq_p[:nw], seq_p[1:]], axis=1)
            it = seq[:, :, None]
            jb = jt[:, None, :]
            mask = (it < jb) | (it > jb + w) | (jb == -1)
            sim = jnp.einsum('bhwie,bhwje->bhwij', bq, bk2) * QK_SCALE
            sim = jnp.where(mask, -jnp.finfo(sim.dtype).max, sim)
            attn = jax.nn.softmax(sim, -1)
            out = jnp.einsum('bhwij,bhwje->bhwie', attn, bv2)
            return out.reshape(b, h, n, d)

        def attn_layer(x, Wqkv, qs, ksc, Wo):
            b, n, _ = x.shape
            qkv = x @ Wqkv
            q, k, v = jnp.split(qkv, 3, -1)
            sh = lambda t: t.reshape(b, n, HEADS, DIM_HEAD).transpose(0, 2, 1, 3)
            q, k, v = (sh(q), sh(k), sh(v))
            q = l2norm(q) * qs
            k = l2norm(k) * ksc
            freqs, scale = rotary_tables(n)
            cos, sin = (jnp.cos(freqs), jnp.sin(freqs))
            q = q * cos * scale + rotate_half(q) * sin * scale
            inv = 1.0 / scale
            k = k * cos * inv + rotate_half(k) * sin * inv
            out = local_attention(q, k, v)
            out = out.transpose(0, 2, 1, 3).reshape(b, n, INNER)
            return out @ Wo

        def ffn_layer(x, g, bln, W1, b1, W2, b2):
            mu = x.mean(-1, keepdims=True)
            var = ((x - mu) ** 2).mean(-1, keepdims=True)
            xn = (x - mu) / jnp.sqrt(var + 1e-05) * g + bln
            hg = xn @ W1 + b1
            a, gate = jnp.split(hg, 2, -1)
            return a * jax.nn.gelu(gate, approximate=False) @ W2 + b2
        key = jax.random.key(seed)
        ks = jax.random.split(key, 8)
        B, N = (2, 256)
        init = lambda k, shape: jax.random.normal(k, shape, jnp.float32) * 0.02
        return {'x': jax.random.normal(ks[0], (B, N, DIM), jnp.float32), 'Wqkv': init(ks[1], (DEPTH, DIM, 3 * INNER)), 'q_scale': jnp.ones((DEPTH, DIM_HEAD), jnp.float32), 'k_scale': jnp.ones((DEPTH, DIM_HEAD), jnp.float32), 'Wo': init(ks[2], (DEPTH, INNER, DIM)), 'ln_g': jnp.ones((DEPTH, DIM), jnp.float32), 'ln_b': jnp.zeros((DEPTH, DIM), jnp.float32), 'W1': init(ks[3], (DEPTH, DIM, 2 * DIM_INNER)), 'b1': jnp.zeros((DEPTH, 2 * DIM_INNER), jnp.float32), 'W2': init(ks[4], (DEPTH, DIM_INNER, DIM)), 'b2': jnp.zeros((DEPTH, DIM), jnp.float32)}
    _L0_ffn_all = _L0_ffn_setup()
    _L0_ffn_in = {k: v for k, v in _L0_ffn_all.items() if k in ('Wqkv', 'q_scale', 'k_scale', 'Wo', 'ln_g', 'ln_b', 'W1', 'b1', 'W2', 'b2')}
    del _L0_ffn_all
    return {'x': x, 'cond_2048': cond_2048, 'L0_cond_W_in': _L0_cond_in['W_in'], 'L0_cond_W_conv': _L0_cond_in['W_conv'], 'L0_cond_b_conv': _L0_cond_in['b_conv'], 'L0_cond_ln_g': _L0_cond_in['ln_g'], 'L0_cond_ln_b': _L0_cond_in['ln_b'], 'L0_cond_W_xproj': _L0_cond_in['W_xproj'], 'L0_cond_W_dt': _L0_cond_in['W_dt'], 'L0_cond_b_dt': _L0_cond_in['b_dt'], 'L0_cond_A_log': _L0_cond_in['A_log'], 'L0_cond_D': _L0_cond_in['D'], 'L0_cond_W_out': _L0_cond_in['W_out'], 'L0_ffn_Wqkv': _L0_ffn_in['Wqkv'], 'L0_ffn_q_scale': _L0_ffn_in['q_scale'], 'L0_ffn_k_scale': _L0_ffn_in['k_scale'], 'L0_ffn_Wo': _L0_ffn_in['Wo'], 'L0_ffn_ln_g': _L0_ffn_in['ln_g'], 'L0_ffn_ln_b': _L0_ffn_in['ln_b'], 'L0_ffn_W1': _L0_ffn_in['W1'], 'L0_ffn_b1': _L0_ffn_in['b1'], 'L0_ffn_W2': _L0_ffn_in['W2'], 'L0_ffn_b2': _L0_ffn_in['b2']}

def reference(x, cond_2048, L0_cond_W_in, L0_cond_W_conv, L0_cond_b_conv, L0_cond_ln_g, L0_cond_ln_b, L0_cond_W_xproj, L0_cond_W_dt, L0_cond_b_dt, L0_cond_A_log, L0_cond_D, L0_cond_W_out, L0_ffn_Wqkv, L0_ffn_q_scale, L0_ffn_k_scale, L0_ffn_Wo, L0_ffn_ln_g, L0_ffn_ln_b, L0_ffn_W1, L0_ffn_b1, L0_ffn_W2, L0_ffn_b2):
    import jax
    import jax.numpy as jnp

    def _L0_cond_ref(x, t_emb, W_in, W_conv, b_conv, ln_g, ln_b, W_xproj, W_dt, b_dt, A_log, D, W_out):
        import jax, jax.numpy as jnp
        import numpy as np
        B, S, D_MODEL, D_INNER, D_STATE = (4, 512, 128, 256, 16)
        d_inner = W_conv.shape[0]
        d_state = A_log.shape[0]
        xr, gate = jnp.split(x @ W_in.T, 2, axis=-1)
        xr = xr + t_emb[:, None, :]
        xc = jax.lax.conv_general_dilated(xr.transpose(0, 2, 1), W_conv, (1,), [(3, 0)], feature_group_count=d_inner, dimension_numbers=('NCH', 'OIH', 'NCH')) + b_conv[None, :, None]
        xc = jax.nn.silu(xc).transpose(0, 2, 1)
        mu = xc.mean(-1, keepdims=True)
        var = xc.var(-1, keepdims=True)
        xn = (xc - mu) / jnp.sqrt(var + 1e-05) * ln_g + ln_b
        Bm, Cm, dt = jnp.split(xn @ W_xproj.T, 3, axis=-1)
        dt = jnp.tanh(dt @ W_dt.T + b_dt) * 0.01
        A = -jnp.tanh(A_log)
        Ad = 1.0 + dt * A
        Bd = Bm * jnp.minimum(jnp.linalg.norm(xn, axis=-1, keepdims=True), 1.0)
        h0 = jnp.zeros((xn.shape[0], d_state, d_inner), xn.dtype)

        def step(h, inputs):
            ad, bd, xt, ct = inputs
            h = jnp.clip(h * ad[:, :, None] + bd[:, :, None] * xt[:, None, :], -10.0, 10.0)
            yt = jnp.einsum('bd,bdh->bh', ct, h)
            return (h, yt)
        _, ys = jax.lax.scan(step, h0, (Ad.transpose(1, 0, 2), Bd.transpose(1, 0, 2), xn.transpose(1, 0, 2), Cm.transpose(1, 0, 2)))
        y = ys.transpose(1, 0, 2) + D * xn
        return y * jax.nn.silu(gate) @ W_out.T

    def _L0_ffn_ref(x, Wqkv, q_scale, k_scale, Wo, ln_g, ln_b, W1, b1, W2, b2):
        import jax, jax.numpy as jnp
        import numpy as np
        DIM = 128
        DEPTH = 6
        HEADS = 16
        DIM_HEAD = 64
        WINDOW = 32
        INNER = HEADS * DIM_HEAD
        DIM_INNER = int(DIM * 4 * 2 / 3)
        QK_SCALE = 8.0

        def shift_tokens(t):
            a, s = jnp.split(t, 2, -1)
            s = jnp.pad(s, ((0, 0), (1, 0), (0, 0)))[:, :-1]
            return jnp.concatenate([a, s], -1)

        def l2norm(t):
            return t / jnp.maximum(jnp.linalg.norm(t, axis=-1, keepdims=True), 1e-12)

        def rotate_half(x):
            x1, x2 = jnp.split(x, 2, -1)
            return jnp.concatenate([-x2, x1], -1)

        def rotary_tables(n):
            half = jnp.arange(0, DIM_HEAD, 2, dtype=jnp.float32)
            inv_freq = 1.0 / 10000.0 ** (half / DIM_HEAD)
            t = jnp.arange(n, dtype=jnp.float32)
            freqs = t[:, None] * inv_freq[None, :]
            freqs = jnp.concatenate([freqs, freqs], -1)
            base_scale = (half + 0.4 * DIM_HEAD) / (1.4 * DIM_HEAD)
            power = (t - n // 2) / (WINDOW // 2)
            scale = base_scale[None, :] ** power[:, None]
            scale = jnp.concatenate([scale, scale], -1)
            return (freqs, scale)

        def local_attention(q, k, v):
            b, h, n, d = q.shape
            w = WINDOW
            nw = n // w
            bq = q.reshape(b, h, nw, w, d)
            bk = k.reshape(b, h, nw, w, d)
            bv = v.reshape(b, h, nw, w, d)

            def look(t):
                p = jnp.pad(t, ((0, 0), (0, 0), (1, 0), (0, 0), (0, 0)))
                return jnp.concatenate([p[:, :, :nw], p[:, :, 1:]], axis=3)
            bk2, bv2 = (look(bk), look(bv))
            seq = jnp.arange(n).reshape(nw, w)
            seq_p = jnp.pad(seq, ((1, 0), (0, 0)), constant_values=-1)
            jt = jnp.concatenate([seq_p[:nw], seq_p[1:]], axis=1)
            it = seq[:, :, None]
            jb = jt[:, None, :]
            mask = (it < jb) | (it > jb + w) | (jb == -1)
            sim = jnp.einsum('bhwie,bhwje->bhwij', bq, bk2) * QK_SCALE
            sim = jnp.where(mask, -jnp.finfo(sim.dtype).max, sim)
            attn = jax.nn.softmax(sim, -1)
            out = jnp.einsum('bhwij,bhwje->bhwie', attn, bv2)
            return out.reshape(b, h, n, d)

        def attn_layer(x, Wqkv, qs, ksc, Wo):
            b, n, _ = x.shape
            qkv = x @ Wqkv
            q, k, v = jnp.split(qkv, 3, -1)
            sh = lambda t: t.reshape(b, n, HEADS, DIM_HEAD).transpose(0, 2, 1, 3)
            q, k, v = (sh(q), sh(k), sh(v))
            q = l2norm(q) * qs
            k = l2norm(k) * ksc
            freqs, scale = rotary_tables(n)
            cos, sin = (jnp.cos(freqs), jnp.sin(freqs))
            q = q * cos * scale + rotate_half(q) * sin * scale
            inv = 1.0 / scale
            k = k * cos * inv + rotate_half(k) * sin * inv
            out = local_attention(q, k, v)
            out = out.transpose(0, 2, 1, 3).reshape(b, n, INNER)
            return out @ Wo

        def ffn_layer(x, g, bln, W1, b1, W2, b2):
            mu = x.mean(-1, keepdims=True)
            var = ((x - mu) ** 2).mean(-1, keepdims=True)
            xn = (x - mu) / jnp.sqrt(var + 1e-05) * g + bln
            hg = xn @ W1 + b1
            a, gate = jnp.split(hg, 2, -1)
            return a * jax.nn.gelu(gate, approximate=False) @ W2 + b2
        for i in range(DEPTH):
            x = attn_layer(shift_tokens(x), Wqkv[i], q_scale[i], k_scale[i], Wo[i]) + x
            x = ffn_layer(shift_tokens(x), ln_g[i], ln_b[i], W1[i], b1[i], W2[i], b2[i]) + x
        return x
    x = x + _L0_ffn_ref(_L0_cond_ref(x, cond_2048, L0_cond_W_in, L0_cond_W_conv, L0_cond_b_conv, L0_cond_ln_g, L0_cond_ln_b, L0_cond_W_xproj, L0_cond_W_dt, L0_cond_b_dt, L0_cond_A_log, L0_cond_D, L0_cond_W_out), L0_ffn_Wqkv, L0_ffn_q_scale, L0_ffn_k_scale, L0_ffn_Wo, L0_ffn_ln_g, L0_ffn_ln_b, L0_ffn_W1, L0_ffn_b1, L0_ffn_W2, L0_ffn_b2)
    return x

_drawn_inputs = setup_inputs


def setup_inputs(seed=0):
    import zlib

    import numpy as np

    out = dict(_drawn_inputs(seed))
    spreads = {'L0_cond_b_conv': (0.0, 0.1),
     'L0_cond_ln_g': (1.0, 0.2),
     'L0_cond_ln_b': (0.0, 0.1),
     'L0_cond_D': (0.10000000149011612, 0.6),
     'L0_ffn_q_scale': (1.0, 0.6),
     'L0_ffn_k_scale': (1.0, 0.6),
     'L0_ffn_ln_g': (1.0, 0.6),
     'L0_ffn_ln_b': (0.0, 0.8),
     'L0_ffn_b1': (0.0, 0.472),
     'L0_ffn_b2': (0.0, 0.1)}
    factors = {'L0_cond_W_dt': 8.0, 'L0_cond_b_dt': 8.0, 'L0_cond_A_log': 8.0}
    for name, (base, spread) in spreads.items():
        noise = np.random.default_rng([zlib.crc32(name.encode()), seed]).standard_normal(out[name].shape)
        drawn = base * np.exp(spread * noise) if base else spread * noise
        out[name] = jnp.asarray(drawn.astype(out[name].dtype))
    for name, factor in factors.items():
        out[name] = (out[name] * factor).astype(out[name].dtype)
    return out
```

```python
from contextlib import ExitStack

import numpy as np

import concourse.bass as bass
from concourse import mybir

F32 = mybir.dt.float32
BF16 = mybir.dt.bfloat16
ALU = mybir.AluOpType
ACT = mybir.ActivationFunctionType
AX = mybir.AxisListType

P = 128
B, S, DM = 128, 32, 128
DI, DS, TAPS = 256, 16, 4
NPROJ = 3 * DS
NB = 4
DEPTH, HEADS, DH = 6, 16, 64
INNER = HEADS * DH
HID = 341
QK_SCALE = 8.0
TOKENS = B * S
TILE_B = P // S
GT = 4
GTOK = GT * P
TILES = TOKENS // P
GROUPS = TILES // GT
NG = DEPTH * GROUPS
NT = NG * GT
HP = HEADS // 2
HBLK = [(0, 128), (128, 128), (256, HID - 256)]
LN_EPS = 1e-5
NORM_SHIFT = 20
NEG = -1e30
ROT_OPS = 6
FFN_DMAS = 10
EXP_LN = "natural_log_exp_and_others"


def wait_for(eng, sem, count):
    if isinstance(count, int) and count <= 0:
        return
    eng.wait_ge(sem, count)


def cond_block(nc, d, res):
    with ExitStack() as ctx:
        def sb(name, shape, dt=F32):
            return ctx.enter_context(nc.sbuf_tensor(name, shape, dt))

        def pb(name, shape):
            return ctx.enter_context(nc.psum_tensor(name, shape, F32))

        def sem(name):
            return ctx.enter_context(nc.semaphore(name))

        ident = sb("c_ident", [P, P])
        win = sb("c_win", [P, 4, DM])
        winT = sb("c_winT", [DM, 4, P])
        wtap = sb("c_wtap", [DM, TAPS, DI])
        wconv = sb("c_wconv", [P, DI, TAPS])
        wx = sb("c_wx", [NPROJ, DI])
        wxdt = sb("c_wxdt", [DS, DI])
        wdtT = sb("c_wdtT", [DS, DS])
        proj_w = sb("c_proj_w", [P, 2, NPROJ])
        wout = sb("c_wout", [DM, DI])
        woutT = sb("c_woutT", [P, 2, DM])
        bconv = sb("c_bconv", [P, DI])
        lng = sb("c_lng", [P, DI])
        lnb = sb("c_lnb", [P, DI])
        dskip = sb("c_dskip", [P, DI])
        bdt = sb("c_bdt", [P, DS])
        alog = sb("c_alog", [P, DS])
        neg_a = sb("c_neg_a", [P, DS])
        temb = sb("c_temb", [P, DI])
        tap_bias = sb("c_tap_bias", [P, TAPS, DI])
        tap_tmp = sb("c_tap_tmp", [P, DI])
        x_ring = sb("c_x_ring", [P, 4, DM])
        xT_ring = sb("c_xT_ring", [DM, 4, P])
        xn = sb("c_xn", [P, S, DI])
        gate = sb("c_gate", [P, S, DI])
        pre = sb("c_pre", [P, 2, DI])
        stats = sb("c_stats", [P, 2, 6])
        mv_t = sb("c_mv_t", [P, 2, 2])
        mv = sb("c_mv", [P, S, 2])
        rstd = sb("c_rstd", [P, S])
        ln_tmp = sb("c_ln_tmp", [P, S])
        u = sb("c_u", [P, 2, DS, DI])
        sqs = u[:, :, 0:NB, :]
        nrm = sb("c_nrm", [P, S])
        eps_c = sb("c_eps", [P, 1])
        pconv = pb("c_pconv", [P, 512])
        pgate = pb("c_pgate", [P, 512])
        ptr = pb("c_ptr", [P, 512])

        w_in_loaded = sem("c_w_in_loaded")
        small_loaded = sem("c_small_loaded")
        x_loaded = [sem(f"c_x_loaded{k}") for k in range(4)]
        set_up = sem("c_set_up")
        set_up_used = sem("c_set_up_used")
        taps_ready = sem("c_taps_ready")
        consts = sem("c_consts")
        chain = sem("c_chain")
        x_transposed = sem("c_x_transposed")
        xT_ready = sem("c_xT_ready")
        oldest_read = sem("c_oldest_read")
        conv_done = sem("c_conv_done")
        gate_done = sem("c_gate_done")
        pre_ready = sem("c_pre_ready")
        silu_done = sem("c_silu_done")
        gate_ready = sem("c_gate_ready")
        stats_done = sem("c_stats_done")
        aggr_done = sem("c_aggr_done")
        mv_done = sem("c_mv_done")
        ln_done = sem("c_ln_done")
        rstd_ready = sem("c_rstd_ready")
        centred = sem("c_centred")
        scaled_done = sem("c_scaled_done")
        shifted = sem("c_shifted")
        sq_done = sem("c_sq_done")
        sums_done = sem("c_sums_done")
        norm_clamped = sem("c_norm_clamped")
        nrm_ready = sem("c_nrm_ready")

        with nc.Block() as block:
            @block.sync
            def _(sp):
                sp.dma_start(ident[:], d["ident"]).then_inc(w_in_loaded, 16)
                sp.dma_start(win[:], d["W_in"].rearrange("(r p) m -> p r m", p=P)).then_inc(w_in_loaded, 16)
                sp.dma_start(wx[:], d["W_xproj"]).then_inc(w_in_loaded, 16)
                sp.dma_start(wout[:], d["W_out"]).then_inc(w_in_loaded, 16)
                sp.dma_start(wxdt[:], d["W_xproj"][2 * DS:NPROJ, :]).then_inc(w_in_loaded, 16)
                sp.dma_start(wdtT[:], d["W_dt"].rearrange("d e -> e d")).then_inc(w_in_loaded, 16)
                for k in range(4):
                    sp.dma_start(x_ring[:, k, :], d["x"][:, k, :]).then_inc(x_loaded[k], 16)
                with sp.Fori(1, S // 4) as i:
                    for k in range(4):
                        sp.wait_ge(x_transposed, i * 4 + k - 3)
                        sp.dma_start(x_ring[:, k, :], d["x"][:, bass.ds(i * 4 + k, 1), :]
                                     .rearrange("b o m -> b (o m)")).then_inc(x_loaded[k], 16)

            @block.gpsimd
            def _(pool):
                pool.memset(eps_c[:], LN_EPS).then_inc(consts, 1)
                pool.memset(xT_ring[:], 0.0).then_inc(consts, 1)
                row = lambda name: d[name].rearrange("(o n) -> o n", o=1)
                pool.dma_start(wconv[:].rearrange("p c k -> p (c k)"),
                               d["W_conv"].rearrange("(o c) i k -> o (c i k)", o=1)
                               .to_broadcast([P, DI * TAPS])).then_inc(small_loaded, 16)
                for tile, name, n in ((bconv, "b_conv", DI), (lng, "ln_g", DI), (lnb, "ln_b", DI), (dskip, "D", DI),
                                      (bdt, "b_dt", DS), (alog, "A_log", DS)):
                    pool.dma_start(tile[:], row(name).to_broadcast([P, n])).then_inc(small_loaded, 16)
                pool.dma_start(temb[:], d["cond"]).then_inc(small_loaded, 16)
                with pool.Fori(0, S // NB) as b:
                    pool.wait_ge(scaled_done, b + 1)
                    x_b = xn[:, bass.ds(b * NB, NB), :]
                    pool.tensor_tensor(x_b, x_b, lnb[:].unsqueeze(1).to_broadcast([P, NB, DI]), ALU.add)\
                        .then_inc(shifted, 1)

            @block.tensor
            def _(pe):
                pe.wait_ge(w_in_loaded, 6 * 16)
                for r in range(4):
                    last = pe.transpose(ptr[:, r * P:(r + 1) * P], win[:, r, :], ident[:])
                last.then_inc(set_up, 1)
                for f in range(2):
                    pe.transpose(pconv[:, f * P:(f + 1) * P], wout[:, f * P:(f + 1) * P], ident[:])
                    last = pe.transpose(pconv[:, 256 + f * NPROJ:256 + (f + 1) * NPROJ], wx[:, f * P:(f + 1) * P],
                                        ident[0:NPROJ, 0:NPROJ])
                last.then_inc(set_up, 1)
                for f in range(2):
                    last = pe.matmul(pgate[:, f * DS:(f + 1) * DS], wxdt[:, f * P:(f + 1) * P], wdtT[:],
                                     start=True, stop=True)
                last.then_inc(set_up, 1)
                pe.wait_ge(set_up_used, 4)
                pe.wait_ge(taps_ready, TAPS)

                def transpose_x(t, k):
                    if isinstance(t, int) and t >= S:
                        return
                    pe.wait_ge(x_loaded[k], (t // 4 + 1) * 16)
                    wait_for(pe, xT_ready, t)
                    pe.transpose(ptr[:, 0:P], x_ring[:, k, :], ident[:]).then_inc(x_transposed, 1)

                def step(t, k, more):
                    pe.wait_ge(xT_ready, t + 1)
                    wait_for(pe, pre_ready, t)
                    for tap in range(TAPS):
                        one = pe.matmul(pconv[:, 0:DI], xT_ring[:, (k + 1 + tap) % 4, :], wtap[:, tap, :],
                                        start=(tap == 0), stop=(tap == TAPS - 1))
                        if tap == 0:
                            one.then_inc(oldest_read, 1)
                    one.then_inc(conv_done, 1)
                    if more:
                        transpose_x(t + 1, (k + 1) % 4)
                    wait_for(pe, gate_ready, t)
                    pe.matmul(pgate[:, 0:DI], xT_ring[:, k, :], winT[:, 2:4, :], start=True, stop=True)\
                        .then_inc(gate_done, 1)

                transpose_x(0, 0)
                for t in range(4):
                    step(t, t, True)
                with pe.Fori(1, S // 4 - 1) as i:
                    for k in range(4):
                        step(i * 4 + k, k, True)
                for t in range(S - 4, S):
                    step(t, t % 4, t + 1 < S)

            @block.scalar
            def _(act):
                act.wait_ge(set_up, 1)
                act.copy(winT[:].rearrange("m r p -> m (r p)"), ptr[:]).then_inc(set_up_used, 1)
                act.wait_ge(set_up, 2)
                act.copy(woutT[:].rearrange("p f m -> p (f m)"), pconv[:, 0:2 * P]).then_inc(set_up_used, 1)
                act.copy(proj_w[:, :, 0:2 * DS],
                         pconv[:, 256:256 + 2 * NPROJ].rearrange("p (f n) -> p f n", f=2)[:, :, 0:2 * DS])\
                    .then_inc(set_up_used, 1)
                act.wait_ge(set_up, 3)
                act.copy(proj_w[:, :, 2 * DS:NPROJ], pgate[:, 0:2 * DS].rearrange("p (f n) -> p f n", f=2))\
                    .then_inc(set_up_used, 1)

                def xT_copy(t, k):
                    act.wait_ge(x_transposed, t + 1)
                    wait_for(act, oldest_read, t)
                    if not isinstance(t, int) or t >= 4:
                        wait_for(act, gate_done, t - 3)
                    act.copy(xT_ring[:, k, :], ptr[:, 0:P]).then_inc(xT_ready, 1)

                def step(t, k, more):
                    if more:
                        xT_copy(t + 1, (k + 1) % 4)
                    act.wait_ge(pre_ready, t + 1)
                    act.activation(xn[:, bass.ds(t, 1), :].rearrange("p o c -> p (o c)"), pre[:, k % 2, :], ACT.Silu)\
                        .then_inc(silu_done, 1)
                    act.wait_ge(gate_done, t + 1)
                    act.activation(gate[:, bass.ds(t, 1), :].rearrange("p o c -> p (o c)"), pgate[:, 0:DI], ACT.Silu)\
                        .then_inc(gate_ready, 1)

                act.wait_ge(consts, 2)
                xT_copy(0, 0)
                for t in range(4):
                    step(t, t, True)
                with act.Fori(1, S // 4 - 1) as i:
                    for k in range(4):
                        step(i * 4 + k, k, True)
                for t in range(S - 4, S):
                    step(t, t % 4, t + 1 < S)
                act.preload_act_table_set(EXP_LN)
                act.wait_ge(mv_done, S)
                act.activation(ln_tmp[:], mv[:, :, 1], ACT.Ln, bias=eps_c[:]).then_inc(ln_done, 1)
                act.wait_ge(ln_done, 1)
                act.activation(rstd[:], ln_tmp[:], ACT.Exp, scale=-0.5).then_inc(rstd_ready, 1)

                def square(b, k):
                    act.wait_ge(shifted, b + 1)
                    wait_for(act, sums_done, b - 1)
                    act.activation(sqs[:, k, :, :], xn[:, bass.ds(b * NB, NB), :], ACT.Square).then_inc(sq_done, 1)

                square(0, 0)
                square(1, 1)
                with act.Fori(1, S // NB // 2) as i:
                    for k in range(2):
                        square(i * 2 + k, k)
                act.wait_ge(norm_clamped, 1)
                act.activation(ln_tmp[:], nrm[:], ACT.Ln).then_inc(ln_done, 1)
                act.wait_ge(ln_done, 2)
                act.activation(nrm[:], ln_tmp[:], ACT.Exp, scale=0.5).then_inc(nrm_ready, 1)
                act.activation(neg_a[:], alog[:], ACT.Tanh).then_inc(nrm_ready, 1)

            @block.vector
            def _(dve):
                dve.wait_ge(small_loaded, 8 * 16)
                dve.wait_ge(set_up_used, 1)
                for k in range(TAPS):
                    dve.tensor_tensor(wtap[:, k, :], winT[:, 0:2, :].rearrange("m r p -> m (r p)"), wconv[:, :, k],
                                      ALU.mult).then_inc(taps_ready, 1)
                done = 0
                for t in range(TAPS):
                    dve.tensor_tensor(tap_tmp[:], temb[:], wconv[:, :, TAPS - 1 - t], ALU.mult).then_inc(chain, 1)
                    done += 1
                    dve.wait_ge(chain, done)
                    dve.tensor_tensor(tap_bias[:, t, :], tap_tmp[:], bconv[:] if t == 0 else tap_bias[:, t - 1, :],
                                      ALU.add).then_inc(chain, 1)
                    done += 1
                    dve.wait_ge(chain, done)

                def statistics(t, k):
                    dve.wait_ge(silu_done, t + 1)
                    wait_for(dve, aggr_done, t - 1)
                    dve.bn_stats(stats[:, k % 2, :], xn[:, bass.ds(t, 1), :].rearrange("p o c -> p (o c)"))\
                        .then_inc(stats_done, 1)
                    dve.wait_ge(stats_done, t + 1)
                    if not isinstance(t, int) or t:
                        keep(t - 1, k - 1)
                    dve.bn_aggr(mv_t[:, k % 2, :], stats[:, k % 2, :]).then_inc(aggr_done, 1)

                def keep(t, k):
                    dve.wait_ge(aggr_done, t + 1)
                    dve.tensor_copy(mv[:, bass.ds(t, 1), :].rearrange("p o c -> p (o c)"), mv_t[:, k % 2, :])\
                        .then_inc(mv_done, 1)

                def step(t, k):
                    dve.wait_ge(conv_done, t + 1)
                    wait_for(dve, silu_done, t - 1)
                    bias = tap_bias[:, min(t, TAPS - 1) if isinstance(t, int) else TAPS - 1, :]
                    dve.tensor_tensor(pre[:, k % 2, :], pconv[:, 0:DI], bias, ALU.add).then_inc(pre_ready, 1)

                for t in range(4):
                    step(t, t)
                    if t:
                        statistics(t - 1, t - 1)
                with dve.Fori(1, S // 4) as i:
                    for k in range(4):
                        step(i * 4 + k, k)
                        statistics(i * 4 + k - 1, (k - 1) % 4)
                statistics(S - 1, (S - 1) % 4)
                keep(S - 1, (S - 1) % 4)
                dve.wait_ge(rstd_ready, 1)

                def scaled(b):
                    for q in range(NB):
                        t = b * NB + q
                        x_t = xn[:, bass.ds(t, 1), :].rearrange("p o c -> p (o c)")
                        dve.tensor_scalar(x_t, x_t, mv[:, bass.ds(t, 1), 0], rstd[:, bass.ds(t, 1)],
                                          ALU.subtract, ALU.mult).then_inc(centred, 1)
                    dve.wait_ge(centred, NB * b + NB)
                    x_b = xn[:, bass.ds(b * NB, NB), :]
                    dve.tensor_tensor(x_b, x_b, lng[:].unsqueeze(1).to_broadcast([P, NB, DI]), ALU.mult)\
                        .then_inc(scaled_done, 1)

                def summed(b, k):
                    dve.wait_ge(sq_done, b + 1)
                    dve.reduce_sum(nrm[:, bass.ds(b * NB, NB)], sqs[:, k, :, :], AX.X).then_inc(sums_done, 1)

                scaled(0)
                scaled(1)
                with dve.Fori(1, S // NB // 2) as i:
                    for k in range(2):
                        scaled(i * 2 + k)
                        summed(i * 2 + k - 2, k)
                for k in range(2):
                    summed(S // NB - 2 + k, k)
                dve.wait_ge(sums_done, S // NB)
                dve.tensor_scalar(nrm[:], nrm[:], 1e-19, 1.0, ALU.max, ALU.min).then_inc(norm_clamped, 1)
                dve.wait_ge(nrm_ready, 2)
                dve.tensor_scalar(neg_a[:], neg_a[:], -0.01, None, ALU.mult).then_inc(chain, 1)

        scan_phase(nc, ctx, sb, sem, pb, dict(ident=ident, xn=xn, gate=gate, nrm=nrm, neg_a=neg_a, proj_w=proj_w,
                                              woutT=woutT, bdt=bdt, dskip=dskip, ptr=ptr, pproj=pgate, res=res, u=u))


def scan_phase(nc, ctx, sb, sem, pb, a):
    ident, xn, gate, nrm, neg_a = a["ident"], a["xn"], a["gate"], a["nrm"], a["neg_a"]
    proj_w, woutT, bdt, dskip, ptr, pproj, res, u = (a[k] for k in "proj_w woutT bdt dskip ptr pproj res u".split())
    NS = DS * DI
    x_now = sb("s_x", [P, 2, DI])
    xnT = sb("s_xnT", [P, 2, P])
    decay = sb("s_decay", [P, 2, DS])
    bd = sb("s_bd", [P, 2, DS])
    cm = sb("s_cm", [P, 2, DS])
    dtp = sb("s_dtp", [P, DS])
    dtt = sb("s_dtt", [P, DS])
    h = sb("s_h", [P, 2, DS, DI])
    cdiag = sb("s_cdiag", [P, 2, DS, P])
    dx = sb("s_dx", [P, 2, DI])
    z = sb("s_z", [P, 2, DI])
    zT = sb("s_zT", [P, 2, P])
    py = [pb(f"s_py{k}", [P, 512]) for k in range(2)]
    pout = pb("s_pout", [P, 512])
    pzT = pb("s_pzT", [P, 512])

    x_copied, xT_done, xT_copied = sem("s_x_copied"), sem("s_xT_done"), sem("s_xT_copied")
    proj_done, proj_read, dt_pre, dt_tanh, decay_ready = (sem(n) for n in (
        "s_proj_done", "s_proj_read", "s_dt_pre", "s_dt_tanh", "s_decay_ready"))
    u_ready, u_read, h_cell, h_ready = sem("s_u_ready"), sem("s_u_read"), sem("s_h_cell"), sem("s_h_ready")
    cdiag_ready, dx_ready, y_done, z_sum, z_ready = (sem(n) for n in (
        "s_cdiag_ready", "s_dx_ready", "s_y_done", "s_z_sum", "s_z_ready"))
    zT_done, zT_copied, out_done, res_written, zeroed = (sem(n) for n in (
        "s_zT_done", "s_zT_copied", "s_out_done", "s_res_written", "s_zeroed"))
    at = lambda buf, t: buf[:, bass.ds(t, 1), :].rearrange("p o c -> p (o c)")
    live = lambda t: not isinstance(t, int) or 0 <= t < S

    def turns(eng, turn):
        for t in range(-2, 4):
            turn(t, t % 2)
        with eng.Fori(2, S // 2 - 1) as i:
            for k in range(2):
                turn(i * 2 + k, k)
        for t in range(S - 2, S + 2):
            turn(t, t % 2)

    with nc.Block() as block:
        @block.tensor
        def _(pe):
            def transpose_x(t, k):
                pe.wait_ge(x_copied, t + 1)
                wait_for(pe, xT_copied, t)
                for f in range(2):
                    last = pe.transpose(ptr[:, f * P:(f + 1) * P], x_now[:, k, f * P:(f + 1) * P], ident[:])
                last.then_inc(xT_done, 1)

            def project(t):
                pe.wait_ge(xT_copied, t + 1)
                wait_for(pe, proj_read, 2 * t)
                wait_for(pe, dt_pre, t)
                for f in range(2):
                    last = pe.matmul(pproj[:, 0:NPROJ], xnT[:, f, :], proj_w[:, f, :], start=(f == 0), stop=(f == 1))
                last.then_inc(proj_done, 1)

            def y_product(t, k):
                pe.wait_ge(cdiag_ready, t + 1)
                pe.wait_ge(h_ready, t + 1)
                wait_for(pe, z_sum, t - 1)
                for s in range(DS):
                    last = pe.matmul(py[k][:, 0:DI], cdiag[:, k, s, :], h[:, k, s, :], start=(s == 0),
                                     stop=(s == DS - 1))
                last.then_inc(y_done, 1)

            def transpose_z(t, k):
                pe.wait_ge(z_ready, t + 1)
                wait_for(pe, zT_copied, t)
                for f in range(2):
                    last = pe.transpose(pzT[:, f * P:(f + 1) * P], z[:, k, f * P:(f + 1) * P], ident[:])
                last.then_inc(zT_done, 1)

            def output(t):
                pe.wait_ge(zT_copied, t + 1)
                wait_for(pe, res_written, t)
                for f in range(2):
                    last = pe.matmul(pout[:, 0:P], woutT[:, f, :], zT[:, f, :], start=(f == 0), stop=(f == 1))
                last.then_inc(out_done, 1)

            def turn(t, k):
                if live(t + 2):
                    transpose_x(t + 2, k)
                if live(t - 2):
                    transpose_z(t - 2, k)
                if live(t + 2):
                    project(t + 2)
                if live(t - 2):
                    output(t - 2)
                if live(t):
                    y_product(t, k)

            turns(pe, turn)

        @block.scalar
        def _(act):
            def outer(t, k):
                act.wait_ge(proj_read, 2 * t + 1)
                act.wait_ge(x_copied, t + 1)
                wait_for(act, h_cell, DS * (t - 1))
                for s in range(DS):
                    act.activation(u[:, k, s, :], x_now[:, k, :], ACT.Copy, scale=bd[:, k, s:s + 1])\
                        .then_inc(u_ready, 1)

            def turn(t, k):
                if live(t + 1):
                    outer(t + 1, 1 - k)
                if live(t + 2):
                    act.wait_ge(xT_done, t + 3)
                    act.copy(xnT[:].rearrange("p f b -> p (f b)"), ptr[:, 0:2 * P]).then_inc(xT_copied, 1)
                if live(t - 2):
                    act.wait_ge(zT_done, t - 1)
                    act.copy(zT[:].rearrange("p f b -> p (f b)"), pzT[:, 0:2 * P]).then_inc(zT_copied, 1)
                    act.wait_ge(out_done, t - 1)
                    act.copy(res[:].rearrange("p (b t) -> p b t", t=S)[:, :, bass.ds(t - 2, 1)],
                             pout[:, 0:P].rearrange("p (b o) -> p b o", o=1)).then_inc(res_written, 1)
                if live(t + 2):
                    act.wait_ge(dt_pre, t + 3)
                    wait_for(act, decay_ready, 2 * (t + 1) + 1)
                    act.activation(dtt[:], dtp[:], ACT.Tanh).then_inc(dt_tanh, 1)

            turns(act, turn)

        @block.gpsimd
        def _(pool):
            pool.memset(h[:, 1, :, :], 0.0).then_inc(zeroed, 1)

            def turn(t, k):
                if live(t):
                    wait_for(pool, z_sum, t - 1)
                    pool.wait_ge(x_copied, t + 1)
                    pool.tensor_tensor(dx[:, k, :], x_now[:, k, :], dskip[:], ALU.mult).then_inc(dx_ready, 1)
                if live(t + 2):
                    wait_for(pool, u_ready, DS * (t + 1))
                    wait_for(pool, xT_done, t + 1)
                    wait_for(pool, dx_ready, t + 1)
                    pool.tensor_copy(x_now[:, k, :], at(xn, t + 2)).then_inc(x_copied, 1)
                if live(t + 1):
                    pool.wait_ge(proj_read, 2 * (t + 1) + 2)
                    wait_for(pool, y_done, t)
                    pool.tensor_tensor(cdiag[:, 1 - k, :, :], ident[:].unsqueeze(1).to_broadcast([P, DS, P]),
                                       cm[:, 1 - k, :].unsqueeze(2).to_broadcast([P, DS, P]), ALU.mult)\
                        .then_inc(cdiag_ready, 1)

            turns(pool, turn)

        @block.vector
        def _(dve):
            def project(t, k):
                dve.wait_ge(proj_done, t + 1)
                wait_for(dve, u_ready, DS * (t - 1))
                dve.tensor_scalar(bd[:, k, :], pproj[:, 0:DS], nrm[:, bass.ds(t, 1)], None, ALU.mult)\
                    .then_inc(proj_read, 1)
                wait_for(dve, cdiag_ready, t - 1)
                dve.tensor_copy(cm[:, k, :], pproj[:, DS:2 * DS]).then_inc(proj_read, 1)
                wait_for(dve, dt_tanh, t)
                dve.tensor_tensor(dtp[:], pproj[:, 2 * DS:NPROJ], bdt[:], ALU.add).then_inc(dt_pre, 1)

            def set_decay(t, k):
                dve.wait_ge(dt_tanh, t + 1)
                dve.tensor_tensor(decay[:, k, :], dtt[:], neg_a[:], ALU.mult).then_inc(decay_ready, 1)
                dve.wait_ge(decay_ready, 2 * t + 1)
                dve.tensor_scalar(decay[:, k, :], decay[:, k, :], 1.0, None, ALU.add).then_inc(decay_ready, 1)

            def scan(t, k):
                dve.wait_ge(decay_ready, 2 * t + 2)
                wait_for(dve, h_ready, t)
                wait_for(dve, y_done, t - 1)
                for s in range(DS):
                    dve.wait_ge(u_ready, DS * t + s + 1)
                    dve.scalar_tensor_tensor(h[:, k, s, :], h[:, 1 - k, s, :], decay[:, k, s:s + 1], u[:, k, s, :],
                                             ALU.mult, ALU.add).then_inc(h_cell, 1)
                dve.wait_ge(h_cell, DS * (t + 1))
                flat = h[:, k, :, :].rearrange("p s c -> p (s c)")
                dve.tensor_scalar(flat, flat, 10.0, -10.0, ALU.min, ALU.max).then_inc(h_ready, 1)

            def gated(t, k):
                dve.wait_ge(y_done, t + 1)
                dve.wait_ge(dx_ready, t + 1)
                wait_for(dve, zT_done, t - 1)
                dve.tensor_tensor(z[:, k, :], py[k][:, 0:DI], dx[:, k, :], ALU.add).then_inc(z_sum, 1)
                dve.wait_ge(z_sum, t + 1)
                dve.tensor_tensor(z[:, k, :], z[:, k, :], at(gate, t), ALU.mult).then_inc(z_ready, 1)

            def turn(t, k):
                if live(t):
                    scan(t, k)
                if live(t + 1):
                    set_decay(t + 1, 1 - k)
                if live(t + 2):
                    project(t + 2, k)
                if live(t - 1):
                    gated(t - 1, 1 - k)

            dve.wait_ge(zeroed, 1)
            turns(dve, turn)


def stack(nc, d, res):
    with ExitStack() as ctx:
        def sb(name, shape, dt=F32):
            return ctx.enter_context(nc.sbuf_tensor(name, shape, dt))

        def pb(name, shape):
            return ctx.enter_context(nc.psum_tensor(name, shape, F32))

        def sem(name):
            return ctx.enter_context(nc.semaphore(name))

        ident = sb("ident_sb", [P, P])
        ident_b = sb("ident_b", [P, P], BF16)
        center = sb("center_sb", [P, P])
        mean = sb("mean_sb", [P, P])
        mask_f = sb("mask_f", [P, HEADS * S])
        mask_b = sb("mask_b", [P, HEADS * S], BF16)
        rot_const = sb("rot_const", [P, 4, DH])
        eps_c = sb("eps_c", [P, 1])
        norm_c = sb("norm_c", [P, 1])

        wqkv = sb("wqkv", [DM, 2, 3 * INNER])
        wo = sb("wo", [P, HP, DM])
        w1 = sb("w1", [DM, 2 * HID])
        w2 = sb("w2", [P, 3, DM])
        b1 = sb("b1", [P, 2, 3])
        ln_par = sb("ln_par", [DM, 3])
        qk_scale = sb("qk_scale", [P, 2, 2, DH])
        rot = sb("rot", [P, 4, DH])

        xs = sb("xs", [DM, GT, P])
        sq = sb("sq", [P, 2, INNER])
        ss = sb("ss", [P, 2, HEADS])
        ln_ss = sb("ln_ss", [P, 2, HEADS])
        qk_n = sb("qk_n", [P, 2, INNER])
        qk_r = sb("qk_r", [P, 2, INNER])
        qk_t = sb("qk_t", [P, 2, INNER])
        qT = sb("qT", [P, HP, P])
        kT = sb("kT", [P, HP, TILE_B, 2, S])
        v = sb("v", [P, GT, INNER])
        top = sb("top", [P, HEADS])
        sm = sb("sm", [P, HEADS * S])
        pr = sb("pr", [P, HEADS * S])
        den = sb("den", [P, HEADS])
        rden = sb("rden", [P, HEADS])
        pT = sb("pT", [P, HEADS, P])
        oT = sb("oT", [P, HP, GT, P])
        fs = sb("fs", [DM, GTOK])
        fc = sb("fc", [DM, GTOK])
        fsq = sb("fsq", [DM, GTOK])
        frs = sb("frs", [DM, GTOK])
        fn = sb("fn", [DM, GTOK])
        gt = sb("gt", [P, 3, GTOK])

        pa = [pb(f"pa{k}", [P, INNER]) for k in range(2)]
        px = pb("px", [P, INNER])
        ps = pb("ps", [P, HEADS * S])
        pg = pb("pg", [P, GTOK])

        names = """const_loaded mask_ready zeroed wqkv_loaded wo_loaded ffn_loaded
            qk_scale_loaded rot_ready xs_ready q_full k_full v_full sq_q sq_k sum_q sum_k clamp_q clamp_k ln_q ln_k inv_q inv_k
            norm_q norm_k cos_q cos_k sin_q sin_k rot_q rot_k tq_done tq_out tk_done tk_out v_out
            scores_done top_done sub_done exp_done den_done rden_done probs_done pT_done pv_done pv_out
            wo_done res_attn fs_ready center_done fc_ready fsq_ready var_done fln_done frs_ready fn_mul fn_ready
            gate_done gate_out gelu_done a_done h_ready w2_done res_ready""".split()
        s = {n: sem(n) for n in names}

        heads = lambda ap: ap.rearrange("p (h e) -> p h e", e=DH)
        halves = lambda ap: ap.rearrange("p (h f e) -> p h f e", f=2, e=DH // 2)
        keys = lambda ap: ap.rearrange("p (h j) -> p h j", j=S)
        over = lambda ap, n: ap.unsqueeze(2).to_broadcast([P, ap.shape[1], n])
        per_head = lambda ap: ap.unsqueeze(1).to_broadcast([P, HEADS, ap.shape[1]])

        def group_steps(eng, body):
            body(0)
            body(1)
            with eng.Fori(2, NG) as i:
                body(i)
            body(NG)
            body(NG + 1)

        class Live:
            def __init__(self, i, j):
                k = i if isinstance(i, int) else 2
                n = k * GT + j
                last = NG if isinstance(i, int) else NG + 9
                nt = last * GT
                self.qkv = n < nt
                self.score = 1 <= n <= nt
                self.pv = 2 <= n <= nt + 1
                self.prev = 1 <= k <= last
                self.prev2 = 2 <= k <= last + 1

        with nc.Block() as block:
            @block.sync
            def _(sp):
                for dst, name in ((ident, "ident"), (center, "center"), (mean, "mean"), (mask_f, "mask")):
                    sp.dma_start(dst[:], d[name]).then_inc(s["const_loaded"], 16)
                sp.dma_start(rot_const[:].rearrange("p a e -> p (a e)"), d["rot"]).then_inc(s["const_loaded"], 16)

                def of(name, l):
                    ap = d[name][bass.ds(l, 1)]
                    return ap.rearrange("o a b -> (o a) b") if len(ap.shape) == 3 else ap

                def load_qkv(l, slot):
                    sp.dma_start(wqkv[:, bass.ds(slot, 1), :].rearrange("p o n -> p (o n)"), of("Wqkv", l))\
                        .then_inc(s["wqkv_loaded"], 16)
                    for c, name in enumerate(("q_scale", "k_scale")):
                        sp.dma_start(qk_scale[:, bass.ds(slot, 1), c, :].rearrange("p o n -> p (o n)"),
                                     of(name, l).to_broadcast([P, DH])).then_inc(s["qk_scale_loaded"], 16)

                def load_wo(l):
                    sp.dma_start(wo[:], of("Wo", l).rearrange("(h p) m -> p h m", p=P)).then_inc(s["wo_loaded"], 16)

                def load_ffn(l):
                    sp.dma_start(w1[:], of("W1", l)).then_inc(s["ffn_loaded"], 16)
                    w2_l, b1_l = of("W2", l), of("b1", l)
                    two = 2 * P
                    sp.dma_start(w2[:, 0:2, :], w2_l[0:two, :].rearrange("(h p) m -> p h m", p=P))\
                        .then_inc(s["ffn_loaded"], 16)
                    sp.dma_start(w2[0:HID - two, 2, :], w2_l[two:HID, :]).then_inc(s["ffn_loaded"], 16)
                    for c in range(2):
                        at = c * HID
                        sp.dma_start(b1[:, c, 0:2], b1_l[:, at:at + two].rearrange("o (h p) -> p (o h)", p=P))\
                            .then_inc(s["ffn_loaded"], 16)
                        sp.dma_start(b1[0:HID - two, c, 2:3], b1_l[:, at + two:at + HID].rearrange("o p -> p o"))\
                            .then_inc(s["ffn_loaded"], 16)
                    for c, name in enumerate(("ffn_ln_g", "ffn_ln_b", "b2")):
                        sp.dma_start(ln_par[:, c:c + 1], of(name, l).rearrange("o p -> p o"))\
                            .then_inc(s["ffn_loaded"], 16)

                load_qkv(0, 0)
                load_wo(0)
                load_ffn(0)
                sp.wait_ge(s["wqkv_loaded"], 16)
                sp.wait_ge(s["qk_scale_loaded"], 32)
                load_qkv(1, 1)

                def next_layer(l):
                    sp.wait_ge(s["wo_done"], l * GROUPS)
                    load_wo(l)
                    sp.wait_ge(s["res_ready"], l * GROUPS + GROUPS)
                    load_ffn(l)

                def layer_after(l):
                    sp.wait_ge(s["v_full"], l * TILES + 1)
                    sp.wait_ge(s["rot_ready"], (l * GROUPS + 1) * ROT_OPS)
                    load_qkv(l + 1, (l + 1) % 2)

                with sp.Fori(1, DEPTH - 1) as l:
                    layer_after(l)
                    next_layer(l)
                next_layer(DEPTH - 1)

            @block.tensor
            def _(pe):
                def qkv(i, j):
                    n = i * GT + j
                    l, u = i // GROUPS, 3 * j
                    pe.wait_ge(s["xs_ready"], 2 * (n + 1))
                    if j == 0:
                        pe.wait_ge(s["wqkv_loaded"], (l + 1) * 16)
                    for c, full, free in ((0, "q_full", ("norm_k", n)), (1, "k_full", ("v_out", n)),
                                          (2, "v_full", ("norm_q", n + 1))):
                        wait_for(pe, s[free[0]], free[1])
                        for half in range(2):
                            at = c * INNER + half * 512
                            last = pe.matmul(pa[(u + c) % 2][:, half * 512:half * 512 + 512], xs[:, j, :],
                                             wqkv[:, bass.ds(l % 2, 1), at:at + 512].rearrange("p o n -> p (o n)"),
                                             start=True, stop=True)
                        last.then_inc(s[full], 1)
                        yield

                def transposes(n, c, ready, free, done):
                    pe.wait_ge(s[ready], n + 1)
                    wait_for(pe, s[free[0]], free[1])
                    for hp in range(HP):
                        last = pe.transpose(px[:, hp * P:(hp + 1) * P], qk_r[:, c, hp * P:(hp + 1) * P], ident[:])
                    last.then_inc(s[done], 1)

                def scores(n):
                    pe.wait_ge(s["tq_out"], n + 1)
                    wait_for(pe, s["sub_done"], n)
                    pe.matmul(ps[:], ident_b[:], mask_b[:], start=True, stop=False, skip_group_check=True)
                    pe.wait_ge(s["tk_out"], 2 * (n + 1))
                    for b in range(TILE_B):
                        rows = slice(b * S, (b + 1) * S)
                        for hp in range(HP):
                            last = pe.matmul(ps[rows, hp * 2 * S:(hp + 1) * 2 * S], qT[:, hp, rows],
                                             kT[:, hp, b, :, :].rearrange("p h j -> p (h j)"), start=False, stop=True,
                                             skip_group_check=True)
                    last.then_inc(s["scores_done"], 1)

                def weigh_values(n, j, scored):
                    pe.wait_ge(s["pT_done"], TILE_B * (n + 1))
                    pe.wait_ge(s["v_out"], n + 1)
                    if scored:
                        pe.wait_ge(s["tk_out"], 2 * (n + 2))
                    else:
                        pe.wait_ge(s["pv_out"], n)
                    for h in range(HEADS):
                        at = (h % 2) * DH
                        last = pe.matmul(px[at:at + DH, (h // 2) * P:(h // 2 + 1) * P],
                                         v[:, (j - 2) % GT, h * DH:(h + 1) * DH], pT[:, h, :], start=True, stop=True,
                                         skip_group_check=True)
                    last.then_inc(s["pv_done"], 1)

                def project_out(g, lo, hi):
                    if lo == 0:
                        pe.wait_ge(s["pv_out"], GT * (g + 1))
                        pe.wait_ge(s["wo_loaded"], (g // GROUPS + 1) * 16)
                        wait_for(pe, s["res_ready"], g + GROUPS)
                    for hp in range(lo, hi):
                        last = pe.matmul(pg[:], wo[:, hp, :], oT[:, hp, :, :].rearrange("p t n -> p (t n)"),
                                         start=(hp == 0), stop=(hp == HP - 1))
                    if hi == HP:
                        last.then_inc(s["wo_done"], 1)

                def subtract_mean(g):
                    pe.wait_ge(s["fs_ready"], 2 * (g + 1))
                    pe.wait_ge(s["res_attn"], g + 1)
                    pe.matmul(pg[:], center[:], fs[:], start=True, stop=True).then_inc(s["center_done"], 1)

                def variance(g):
                    pe.wait_ge(s["fsq_ready"], g + 1)
                    pe.matmul(pg[:], mean[:], fsq[:], start=True, stop=True).then_inc(s["var_done"], 1)

                def gate_block(g, k):
                    if k == 0:
                        pe.wait_ge(s["fn_ready"], g + 1)
                        pe.wait_ge(s["ffn_loaded"], (g // GROUPS + 1) * FFN_DMAS * 16)
                    else:
                        pe.wait_ge(s["gate_out"], 3 * g + k)
                    at, m = HBLK[k]
                    pe.matmul(pg[0:m, :], w1[:, HID + at:HID + at + m], fn[:], start=True, stop=True)\
                        .then_inc(s["gate_done"], 1)

                def a_block(g, k):
                    if k == 0:
                        pe.wait_ge(s["gate_out"], 3 * g + 3)
                    else:
                        pe.wait_ge(s["h_ready"], 3 * g + k)
                    at, m = HBLK[k]
                    pe.matmul(pg[0:m, :], w1[:, at:at + m], fn[:], start=True, stop=True).then_inc(s["a_done"], 1)

                def down(g):
                    pe.wait_ge(s["h_ready"], 3 * g + 3)
                    for k, (at, m) in enumerate(HBLK):
                        last = pe.matmul(pg[:], w2[0:m, k, :], gt[0:m, k, :], start=(k == 0), stop=(k == 2))
                    last.then_inc(s["w2_done"], 1)

                def body(i):
                    for j in range(GT):
                        n, live = i * GT + j, Live(i, j)
                        part = qkv(i, j) if live.qkv else iter(())
                        extra = {
                            0: [live.prev2 and (lambda k=k: gate_block(i - 2, k)) for k in range(3)],
                            1: [live.prev2 and (lambda k=k: a_block(i - 2, k)) for k in range(3)],
                            2: [live.prev2 and (lambda: down(i - 2)), live.prev and (lambda: project_out(i - 1, 0, 3)),
                                live.prev and (lambda: project_out(i - 1, 3, 6)),
                                live.prev and (lambda: project_out(i - 1, 6, HP))],
                            3: [None, live.prev and (lambda: subtract_mean(i - 1)), None,
                                live.prev and (lambda: variance(i - 1))],
                        }[j]
                        slot = lambda k: extra[k]() if k < len(extra) and extra[k] else None
                        next(part, None)
                        if live.score:
                            transposes(n - 1, 0, "rot_q", ("pv_out", n - 2), "tq_done")
                        slot(0)
                        next(part, None)
                        if live.score:
                            transposes(n - 1, 1, "rot_k", ("tq_out", n), "tk_done")
                        slot(1)
                        next(part, None)
                        if live.score:
                            scores(n - 1)
                        slot(2)
                        slot(3)
                        if live.pv:
                            weigh_values(n - 2, j, live.score)

                pe.wait_ge(s["const_loaded"], 5 * 16)
                pe.wait_ge(s["mask_ready"], 2)
                pe.wait_ge(s["zeroed"], 7)
                group_steps(pe, body)

            @block.scalar
            def _(act):
                def square(c, k, full, n, sq_sem, sum_sem):
                    act.wait_ge(s[full], n + 1)
                    wait_for(act, s[sum_sem], n)
                    act.activation(sq[:, c, :], pa[k][:], ACT.Square).then_inc(s[sq_sem], 1)

                def inverse_norm(c, n, clamp, ln, inv):
                    act.wait_ge(s[clamp], n + 1)
                    act.activation(ln_ss[:, c, :], ss[:, c, :], ACT.Ln).then_inc(s[ln], 1)
                    act.wait_ge(s[ln], n + 1)
                    act.activation(ss[:, c, :], ln_ss[:, c, :], ACT.Exp, scale=-0.5, bias=norm_c[:])\
                        .then_inc(s[inv], 1)

                def gate_bias(g, k):
                    m = HBLK[k][1]
                    act.wait_ge(s["gate_done"], 3 * g + k + 1)
                    act.activation(gt[0:m, k, :], pg[0:m, :], ACT.Identity, bias=b1[0:m, 1, k:k + 1])\
                        .then_inc(s["gate_out"], 1)

                def body(i):
                    for j in range(GT):
                        n, live = i * GT + j, Live(i, j)
                        u = 3 * j
                        if live.qkv:
                            square(0, u % 2, "q_full", n, "sq_q", "sum_q")
                        if live.score:
                            act.wait_ge(s["tq_done"], n)
                            act.copy(qT[:].rearrange("p h n -> p (h n)"), px[:]).then_inc(s["tq_out"], 1)
                        if live.prev2 and j == 0:
                            gate_bias(i - 2, 0)
                        if live.qkv:
                            inverse_norm(0, n, "clamp_q", "ln_q", "inv_q")
                            square(1, (u + 1) % 2, "k_full", n, "sq_k", "sum_k")
                        if live.score:
                            act.wait_ge(s["tk_done"], n)
                            for half in range(2):
                                rows = slice(half * DH, (half + 1) * DH)
                                act.copy(kT[rows, :, :, half, :].rearrange("p h b j -> p (h b) j"),
                                         px[rows, :].rearrange("p (h j) -> p h j", j=S)).then_inc(s["tk_out"], 1)
                        if live.prev and j == 3:
                            act.wait_ge(s["center_done"], i)
                            act.copy(fc[:], pg[:]).then_inc(s["fc_ready"], 1)
                            act.wait_ge(s["fc_ready"], i)
                            act.activation(fsq[:], fc[:], ACT.Square).then_inc(s["fsq_ready"], 1)
                        if live.prev2 and j == 0:
                            gate_bias(i - 2, 1)
                        if live.qkv:
                            inverse_norm(1, n, "clamp_k", "ln_k", "inv_k")
                            act.wait_ge(s["v_full"], n + 1)
                            act.copy(v[:, j, :], pa[(u + 2) % 2][:]).then_inc(s["v_out"], 1)
                        if live.prev2 and j == 0:
                            gate_bias(i - 2, 2)
                        if live.score:
                            act.wait_ge(s["sub_done"], n)
                            act.activation(pr[:], sm[:], ACT.Exp, scale=QK_SCALE).then_inc(s["exp_done"], 1)
                        if live.prev2 and j == 0:
                            act.wait_ge(s["gate_out"], 3 * (i - 1))
                            act.activation(gt[:], gt[:], ACT.Gelu).then_inc(s["gelu_done"], 1)
                            act.preload_act_table_set(EXP_LN)
                        if live.prev and j == 3:
                            act.wait_ge(s["var_done"], i)
                            act.activation(frs[:], pg[:], ACT.Ln, bias=eps_c[:]).then_inc(s["fln_done"], 1)
                            act.wait_ge(s["fln_done"], i)
                            act.activation(frs[:], frs[:], ACT.Exp, scale=-0.5).then_inc(s["frs_ready"], 1)
                        if live.pv:
                            act.wait_ge(s["pv_done"], n - 1)
                            if j == 2 and live.prev:
                                act.wait_ge(s["wo_done"], i)
                            act.copy(oT[:, :, (j - 2) % GT, :], px[:].rearrange("p (h n) -> p h n", n=P))\
                                .then_inc(s["pv_out"], 1)

                act.preload_act_table_set(EXP_LN)
                act.wait_ge(s["zeroed"], 7)
                group_steps(act, body)

            @block.vector
            def _(dve):
                def sum_squares(c, n, sq_sem, sum_sem, clamp, inv):
                    dve.wait_ge(s[sq_sem], n + 1)
                    wait_for(dve, s[inv], n)
                    dve.reduce_sum(ss[:, c, :], heads(sq[:, c, :]), AX.X).then_inc(s[sum_sem], 1)
                    dve.wait_ge(s[sum_sem], n + 1)
                    dve.tensor_scalar(ss[:, c, :], ss[:, c, :], 2.0 ** NORM_SHIFT, 1e-24 * 2.0 ** NORM_SHIFT,
                                      ALU.mult, ALU.max).then_inc(s[clamp], 1)

                def normalise(c, k, n, inv, sin, norm):
                    dve.wait_ge(s[inv], n + 1)
                    wait_for(dve, s[sin], 2 * n)
                    dve.tensor_tensor(heads(qk_n[:, c, :]), heads(pa[k][:]), over(ss[:, c, :], DH), ALU.mult)\
                        .then_inc(s[norm], 1)

                def times_cos(c, i, n, norm, done, cos):
                    dve.wait_ge(s[norm], n + 1)
                    dve.wait_ge(s["rot_ready"], ROT_OPS * (i + 1))
                    wait_for(dve, s[done], n)
                    dve.tensor_tensor(heads(qk_r[:, c, :]), heads(qk_n[:, c, :]), per_head(rot[:, 2 * c, :]), ALU.mult)\
                        .then_inc(s[cos], 1)

                def gated(g, k):
                    m = HBLK[k][1]
                    if k == 0:
                        dve.wait_ge(s["gelu_done"], g + 1)
                    dve.wait_ge(s["a_done"], 3 * g + k + 1)
                    dve.scalar_tensor_tensor(gt[0:m, k, :], pg[0:m, :], b1[0:m, 0, k:k + 1], gt[0:m, k, :],
                                             ALU.add, ALU.mult).then_inc(s["h_ready"], 1)

                def body(i):
                    for j in range(GT):
                        n, live = i * GT + j, Live(i, j)
                        u = 3 * j
                        if live.qkv:
                            sum_squares(0, n, "sq_q", "sum_q", "clamp_q", "inv_q")
                        if live.pv:
                            dve.wait_ge(s["exp_done"], n - 1)
                            dve.reduce_sum(den[:], keys(pr[:]), AX.X).then_inc(s["den_done"], 1)
                            dve.wait_ge(s["den_done"], n - 1)
                            dve.reciprocal(rden[:], den[:]).then_inc(s["rden_done"], 1)
                        if live.qkv:
                            normalise(0, u % 2, n, "inv_q", "sin_q", "norm_q")
                        if live.prev2 and j == 2:
                            dve.wait_ge(s["w2_done"], i - 1)
                            r = res[:, bass.ds((i - 2) % GROUPS * GTOK, GTOK)]
                            dve.scalar_tensor_tensor(r, pg[:], ln_par[:, 2:3], r, ALU.add, ALU.add)\
                                .then_inc(s["res_ready"], 1)
                        if live.prev2 and j == 1:
                            gated(i - 2, 0)
                        if live.qkv:
                            sum_squares(1, n, "sq_k", "sum_k", "clamp_k", "inv_k")
                            times_cos(0, i, n, "norm_q", "tq_done", "cos_q")
                            normalise(1, (u + 1) % 2, n, "inv_k", "sin_k", "norm_k")
                        if live.pv:
                            dve.wait_ge(s["probs_done"], n - 1)
                            wait_for(dve, s["pv_done"], n - 2)
                            for b in range(TILE_B):
                                rows = slice(b * S, (b + 1) * S)
                                dve.transpose(pT[rows, :, rows], pr[rows, :]).then_inc(s["pT_done"], 1)
                        if live.prev2 and j == 1:
                            gated(i - 2, 1)
                        if live.qkv:
                            times_cos(1, i, n, "norm_k", "tk_done", "cos_k")
                        if live.prev2 and j == 1:
                            gated(i - 2, 2)
                        if live.score:
                            dve.wait_ge(s["scores_done"], n)
                            dve.tensor_reduce(top[:], keys(ps[:]), AX.X, ALU.max).then_inc(s["top_done"], 1)
                            dve.wait_ge(s["top_done"], n)
                            wait_for(dve, s["exp_done"], n - 1)
                            dve.tensor_tensor(keys(sm[:]), keys(ps[:]), over(top[:], S), ALU.subtract)\
                                .then_inc(s["sub_done"], 1)
                        if live.prev and j == 2:
                            dve.wait_ge(s["wo_done"], i)
                            r = res[:, bass.ds((i - 1) % GROUPS * GTOK, GTOK)]
                            dve.tensor_tensor(r, pg[:], r, ALU.add).then_inc(s["res_attn"], 1)
                        if live.prev and j == 3:
                            dve.wait_ge(s["frs_ready"], i)
                            if not isinstance(i, int) or i >= 2:
                                dve.wait_ge(s["a_done"], 3 * (i - 1))
                            dve.wait_ge(s["ffn_loaded"], ((i - 1) // GROUPS + 1) * FFN_DMAS * 16)
                            dve.tensor_tensor(fn[:], fc[:], frs[:], ALU.mult).then_inc(s["fn_mul"], 1)
                            dve.wait_ge(s["fn_mul"], i)
                            dve.tensor_scalar(fn[:], fn[:], ln_par[:, 0:1], ln_par[:, 1:2], ALU.mult, ALU.add)\
                                .then_inc(s["fn_ready"], 1)

                dve.memset(eps_c[:], LN_EPS).then_inc(s["zeroed"], 1)
                dve.memset(norm_c[:], 0.5 * NORM_SHIFT * float(np.log(2.0))).then_inc(s["zeroed"], 1)
                dve.memset(gt[:], 0.0).then_inc(s["zeroed"], 1)
                dve.wait_ge(s["const_loaded"], 5 * 16)
                dve.tensor_copy(ident_b[:], ident[:]).then_inc(s["mask_ready"], 1)
                dve.tensor_copy(mask_b[:], mask_f[:]).then_inc(s["mask_ready"], 1)
                dve.memset(top[:], 0.0).then_inc(s["res_ready"], GROUPS)
                group_steps(dve, body)

            @block.gpsimd
            def _(pool):
                def shift(n, j):
                    if isinstance(n, int) and n >= NT:
                        return
                    at = (n % TILES) * P
                    pool.wait_ge(s["res_ready"], n // GT + 1)
                    if not isinstance(n, int) or n >= GT:
                        pool.wait_ge(s["v_full"], n - GT + 1)
                    pool.tensor_copy(xs[0:64, j, :], res[0:64, bass.ds(at, P)]).then_inc(s["xs_ready"], 1)
                    pool.wait_ge(s["xs_ready"], 2 * n + 1)
                    late(xs[64:P, j, :], res[64:P, bass.ds(at, P)]).then_inc(s["xs_ready"], 1)
                    pool.wait_ge(s["xs_ready"], 2 * n + 2)

                def late(dst, src):
                    dst = dst.rearrange("p (b t) -> p b t", t=S)
                    src = src.rearrange("p (b t) -> p b t", t=S)
                    return pool.tensor_copy(dst[:, :, 1:S], src[:, :, 0:S - 1])

                def rotate(c, n, norm, cos, sin, rot_done, tr):
                    pool.wait_ge(s[norm], n + 1)
                    wait_for(pool, s[rot_done], n)
                    src, dst = halves(qk_n[:, c, :]), halves(qk_t[:, c, :])
                    table = rot[:, 2 * c + 1, :].rearrange("p (f e) -> p f e", f=2)
                    for f in range(2):
                        pool.tensor_tensor(dst[:, :, f, :], src[:, :, 1 - f, :],
                                           table[:, f, :].unsqueeze(1).to_broadcast([P, HEADS, DH // 2]), ALU.mult)\
                            .then_inc(s[sin], 1)
                    pool.wait_ge(s[sin], 2 * n + 2)
                    pool.wait_ge(s[cos], n + 1)
                    pool.tensor_tensor(qk_r[:, c, :], qk_r[:, c, :], qk_t[:, c, :], ALU.add).then_inc(s[rot_done], 1)

                def body(i):
                    for j in range(GT):
                        n, live = i * GT + j, Live(i, j)
                        if live.qkv and j == 0:
                            l = i // GROUPS
                            pool.wait_ge(s["qk_scale_loaded"], 32 * (l + 1))
                            wait_for(pool, s["cos_k"], n)
                            wait_for(pool, s["sin_k"], 2 * n)
                            for c in range(2):
                                sc = qk_scale[:, bass.ds(l % 2, 1), c, :].rearrange("p o e -> p (o e)")
                                pool.tensor_tensor(rot[:, 2 * c, :], rot_const[:, 2 * c, :], sc, ALU.mult)\
                                    .then_inc(s["rot_ready"], 1)
                                for f in range(2):
                                    to, frm = slice(f * DH // 2, (f + 1) * DH // 2), slice((1 - f) * DH // 2, (2 - f) * DH // 2)
                                    pool.tensor_tensor(rot[:, 2 * c + 1, to], rot_const[:, 2 * c + 1, to], sc[:, frm],
                                                       ALU.mult).then_inc(s["rot_ready"], 1)
                            pool.wait_ge(s["rot_ready"], ROT_OPS * (i + 1))
                        if live.pv:
                            pool.wait_ge(s["rden_done"], n - 1)
                            pool.tensor_tensor(keys(pr[:]), keys(pr[:]), over(rden[:], S), ALU.mult)\
                                .then_inc(s["probs_done"], 1)
                        if live.qkv:
                            rotate(0, n, "norm_q", "cos_q", "sin_q", "rot_q", "tq_done")
                            if j < GT - 1:
                                shift(n + 1, j + 1)
                            elif not isinstance(i, int) or i < NG - 1:
                                shift(n + 1, 0)
                            rotate(1, n, "norm_k", "cos_k", "sin_k", "rot_k", "tk_done")
                        if live.prev and j == 2:
                            at = (i - 1) % GROUPS * GTOK
                            pool.wait_ge(s["res_attn"], i)
                            pool.tensor_copy(fs[0:64, :], res[0:64, bass.ds(at, GTOK)]).then_inc(s["fs_ready"], 1)
                            pool.wait_ge(s["fs_ready"], 2 * i - 1)
                            late(fs[64:P, :], res[64:P, bass.ds(at, GTOK)]).then_inc(s["fs_ready"], 1)
                            pool.wait_ge(s["fs_ready"], 2 * i)

                pool.memset(kT[:], 0.0).then_inc(s["zeroed"], 1)
                pool.memset(pT[:], 0.0).then_inc(s["zeroed"], 1)
                pool.memset(xs[:], 0.0).then_inc(s["zeroed"], 1)
                pool.memset(fs[:], 0.0).then_inc(s["zeroed"], 1)
                pool.wait_ge(s["zeroed"], 7)
                pool.wait_ge(s["const_loaded"], 5 * 16)
                shift(0, 0)
                group_steps(pool, body)



def add_input(nc, d, res):
    with ExitStack() as ctx:
        def sb(name, shape):
            return ctx.enter_context(nc.sbuf_tensor(name, shape, F32))

        def sem(name):
            return ctx.enter_context(nc.semaphore(name))

        ident = sb("o_ident", [P, P])
        x_in = sb("o_x", [P, 2, GT, DM])
        src = sb("o_src", [DM, 2, GTOK])
        out = sb("o_out", [P, 2, GT, DM])
        pt = [ctx.enter_context(nc.psum_tensor(f"o_pt{k}", [P, GTOK], F32)) for k in range(2)]
        loaded, src_ready, turned, added = sem("o_loaded"), sem("o_src_ready"), sem("o_turned"), sem("o_added")
        x_loaded = [sem(f"o_x_loaded{k}") for k in range(2)]
        stored = [sem(f"o_stored{k}") for k in range(2)]
        view = lambda ap: ap.rearrange("b t m -> (b t) m").rearrange("(g k p) m -> g p k m", k=GT, p=P)
        x_v, out_v = view(d["x"]), view(d["out"])
        one = lambda ap, g: ap[bass.ds(g, 1)].rearrange("o p k m -> (o p) k m")

        with nc.Block() as block:
            @block.sync
            def _(sp):
                sp.dma_start(ident[:], d["ident"]).then_inc(loaded, 16)

                def load(g, k):
                    wait_for(sp, added, g - 1)
                    sp.dma_start(x_in[:, k], one(x_v, g)).then_inc(x_loaded[k], 16)

                def store(g, k):
                    sp.wait_ge(added, g + 1)
                    sp.dma_start(one(out_v, g), out[:, k]).then_inc(stored[k], 16)

                load(0, 0)
                load(1, 1)
                with sp.Fori(1, GROUPS // 2) as i:
                    for k in range(2):
                        store(i * 2 + k - 2, k)
                        load(i * 2 + k, k)
                for k in range(2):
                    store(GROUPS - 2 + k, k)
                for k in range(2):
                    sp.wait_ge(stored[k], 16 * GROUPS // 2)

            @block.scalar
            def _(act):
                def body(g, k):
                    wait_for(act, turned, g - 1)
                    act.copy(src[:, k, :], res[:, bass.ds(g * GTOK, GTOK)]).then_inc(src_ready, 1)

                body(0, 0)
                body(1, 1)
                with act.Fori(1, GROUPS // 2) as i:
                    for k in range(2):
                        body(i * 2 + k, k)

            @block.tensor
            def _(pe):
                pe.wait_ge(loaded, 16)

                def body(g, k):
                    pe.wait_ge(src_ready, g + 1)
                    wait_for(pe, added, g - 1)
                    for c in range(GT):
                        last = pe.transpose(pt[k][:, c * P:(c + 1) * P], src[:, k, c * P:(c + 1) * P], ident[:])
                    last.then_inc(turned, 1)

                body(0, 0)
                body(1, 1)
                with pe.Fori(1, GROUPS // 2) as i:
                    for k in range(2):
                        body(i * 2 + k, k)

            @block.vector
            def _(dve):
                def body(g, k, i):
                    dve.wait_ge(turned, g + 1)
                    dve.wait_ge(x_loaded[k], 16 * (i + 1))
                    wait_for(dve, stored[k], 16 * i)
                    dve.tensor_tensor(out[:, k].rearrange("p c m -> p (c m)"), pt[k][:],
                                      x_in[:, k].rearrange("p c m -> p (c m)"), ALU.add).then_inc(added, 1)

                body(0, 0, 0)
                body(1, 1, 0)
                with dve.Fori(1, GROUPS // 2) as i:
                    for k in range(2):
                        body(i * 2 + k, k, i)


def build(nc, d):
    with ExitStack() as ctx:
        ctx.enter_context(nc.allow_non_contiguous_dma(reason="small parameters laid out as columns"))
        res = ctx.enter_context(nc.sbuf_tensor("res", [DM, TOKENS], F32))
        cond_block(nc, d, res)
        stack(nc, d, res)
        add_input(nc, d, res)


_INS = {
    "x": "x", "cond_2048": "cond", "L0_cond_W_in": "W_in", "L0_cond_W_conv": "W_conv", "L0_cond_b_conv": "b_conv",
    "L0_cond_ln_g": "ln_g", "L0_cond_ln_b": "ln_b", "L0_cond_W_xproj": "W_xproj", "L0_cond_W_dt": "W_dt",
    "L0_cond_b_dt": "b_dt", "L0_cond_A_log": "A_log", "L0_cond_D": "D", "L0_cond_W_out": "W_out",
    "L0_ffn_Wqkv": "Wqkv", "L0_ffn_q_scale": "q_scale", "L0_ffn_k_scale": "k_scale", "L0_ffn_Wo": "Wo",
    "L0_ffn_ln_g": "ffn_ln_g", "L0_ffn_ln_b": "ffn_ln_b", "L0_ffn_W1": "W1", "L0_ffn_b1": "b1", "L0_ffn_W2": "W2",
    "L0_ffn_b2": "b2",
}


def _shape_constants():
    f = np.float32
    eye = np.eye(P, dtype=f)
    mean = np.full((P, P), 1.0 / DM, f)
    q, k = np.arange(P)[:, None] % S, np.arange(HEADS * S)[None, :] % S
    mask = np.where(k <= q, f(0), f(NEG))
    half = np.arange(0, DH, 2, dtype=f)
    inv_freq = f(1) / np.power(f(10000), half / f(DH))
    t = np.arange(S, dtype=f)
    freqs = t[:, None] * inv_freq[None, :]
    scale = ((half + f(0.4 * DH)) / f(1.4 * DH))[None, :] ** ((t - f(S // 2)) / f(S // 2))[:, None]
    cos, sin = np.cos(freqs), np.sin(freqs)
    row = lambda a, b: np.concatenate([a, b], -1)
    rot = np.concatenate([row(cos * scale, cos * scale), row(-sin * scale, sin * scale),
                          row(cos / scale, cos / scale), row(-sin / scale, sin / scale)], -1)
    rot = np.tile(rot, (P // S, 1))
    return {"ident": eye, "center": eye - mean, "mean": mean, "mask": mask.astype(f), "rot": rot.astype(f)}


def kernel(**inputs):
    import concourse.bacc as bacc
    from concourse.bass_utils import run_bass_kernel_spmd

    nc = bacc.Bacc("TRN2", target_bir_lowering=False, num_devices=1)
    arrays = {short: np.ascontiguousarray(inputs[name]) for name, short in _INS.items()}
    arrays.update(_shape_constants())
    d, maps = {}, {}
    for name, a in arrays.items():
        maps[f"in_{name}"] = a
        d[name] = nc.dram_tensor(f"in_{name}", a.shape, mybir.dt.from_np(a.dtype), kind="ExternalInput").ap()
    d["out"] = nc.dram_tensor("out_0", (B, S, DM), F32, kind="ExternalOutput").ap()
    build(nc, d)
    r = run_bass_kernel_spmd(nc, [maps], core_ids=[0])
    return r.results[0]["out_0"]
```

```python
from contextlib import ExitStack

import numpy as np

import concourse.bass as bass
from concourse import mybir

F32 = mybir.dt.float32
BF16 = mybir.dt.bfloat16
F32R = mybir.dt.float32r
ALU = mybir.AluOpType
ACT = mybir.ActivationFunctionType
AX = mybir.AxisListType

P = 128
B, S, DM = 128, 32, 128
DI, DS, TAPS = 256, 16, 4
NPROJ = 3 * DS
PS = 3
NB = 4
DEPTH, HEADS, DH = 6, 16, 64
INNER = HEADS * DH
HID = 341
QK_SCALE = 8.0
TOKENS = B * S
TILE_B = P // S
GT = 4
GTOK = GT * P
TILES = TOKENS // P
GROUPS = TILES // GT
NG = DEPTH * GROUPS
NT = NG * GT
HP = HEADS // 2
HBLK = [(0, 128), (128, 128), (256, HID - 256)]
LN_EPS = 1e-5
NORM_SHIFT = 20
NEG = -1e30
ROT_OPS = 6
FFN_DMAS = 10
EXP_LN = "natural_log_exp_and_others"


def wait_for(eng, sem, count):
    if isinstance(count, int) and count <= 0:
        return
    eng.wait_ge(sem, count)


def cond_block(nc, d, res):
    with ExitStack() as ctx:
        def sb(name, shape, dt=F32):
            return ctx.enter_context(nc.sbuf_tensor(name, shape, dt))

        def pb(name, shape):
            return ctx.enter_context(nc.psum_tensor(name, shape, F32))

        def sem(name):
            return ctx.enter_context(nc.semaphore(name))

        ident = sb("c_ident", [P, P])
        win = sb("c_win", [P, 4, DM])
        winT = sb("c_winT", [DM, 4, P])
        wtap = sb("c_wtap", [DM, TAPS, DI])
        wconv = sb("c_wconv", [P, DI, TAPS])
        wx = sb("c_wx", [NPROJ, DI])
        wxdt = sb("c_wxdt", [DS, DI])
        wdtT = sb("c_wdtT", [DS, DS])
        proj_w = sb("c_proj_w", [P, 2, NPROJ])
        wout = sb("c_wout", [DM, DI])
        woutT = sb("c_woutT", [P, 2, DM])
        bconv = sb("c_bconv", [P, DI])
        lng = sb("c_lng", [P, DI])
        lnb = sb("c_lnb", [P, DI])
        dskip = sb("c_dskip", [P, DI])
        bdt = sb("c_bdt", [P, DS])
        alog = sb("c_alog", [P, DS])
        neg_a = sb("c_neg_a", [P, DS])
        temb = sb("c_temb", [P, DI])
        tap_bias = sb("c_tap_bias", [P, TAPS, DI])
        tap_tmp = sb("c_tap_tmp", [P, DI])
        x_ring = sb("c_x_ring", [P, 4, DM])
        xT_ring = sb("c_xT_ring", [DM, 4, P])
        xn = sb("c_xn", [P, S, DI])
        gate = sb("c_gate", [P, S, DI])
        pre = sb("c_pre", [P, 2, DI])
        stats = sb("c_stats", [P, 2, 6])
        mv_t = sb("c_mv_t", [P, 2, 2])
        mv = sb("c_mv", [P, S, 2])
        rstd = sb("c_rstd", [P, S])
        ln_tmp = sb("c_ln_tmp", [P, S])
        u = sb("c_u", [P, 2, DS, DI])
        sqs = u[:, :, 0:NB, :]
        nrm = sb("c_nrm", [P, S])
        eps_c = sb("c_eps", [P, 1])
        pconv = pb("c_pconv", [P, 512])
        pgate = pb("c_pgate", [P, 512])
        ptr = pb("c_ptr", [P, 512])

        w_in_loaded = sem("c_w_in_loaded")
        small_loaded = sem("c_small_loaded")
        x_loaded = [sem(f"c_x_loaded{k}") for k in range(4)]
        set_up = sem("c_set_up")
        set_up_used = sem("c_set_up_used")
        taps_ready = sem("c_taps_ready")
        consts = sem("c_consts")
        chain = sem("c_chain")
        x_transposed = sem("c_x_transposed")
        xT_ready = sem("c_xT_ready")
        oldest_read = sem("c_oldest_read")
        conv_done = sem("c_conv_done")
        gate_done = sem("c_gate_done")
        pre_ready = sem("c_pre_ready")
        silu_done = sem("c_silu_done")
        gate_ready = sem("c_gate_ready")
        stats_done = sem("c_stats_done")
        aggr_done = sem("c_aggr_done")
        mv_done = sem("c_mv_done")
        ln_done = sem("c_ln_done")
        rstd_ready = sem("c_rstd_ready")
        centred = sem("c_centred")
        scaled_done = sem("c_scaled_done")
        shifted = sem("c_shifted")
        sq_done = sem("c_sq_done")
        sums_done = sem("c_sums_done")
        norm_clamped = sem("c_norm_clamped")
        nrm_ready = sem("c_nrm_ready")

        with nc.Block() as block:
            @block.sync
            def _(sp):
                sp.dma_start(ident[:], d["ident"]).then_inc(w_in_loaded, 16)
                sp.dma_start(win[:], d["W_in"].rearrange("(r p) m -> p r m", p=P)).then_inc(w_in_loaded, 16)
                sp.dma_start(wx[:], d["W_xproj"]).then_inc(w_in_loaded, 16)
                sp.dma_start(wout[:], d["W_out"]).then_inc(w_in_loaded, 16)
                sp.dma_start(wxdt[:], d["W_xproj"][2 * DS:NPROJ, :]).then_inc(w_in_loaded, 16)
                sp.dma_start(wdtT[:], d["W_dt"].rearrange("d e -> e d")).then_inc(w_in_loaded, 16)
                for k in range(4):
                    sp.dma_start(x_ring[:, k, :], d["x"][:, k, :]).then_inc(x_loaded[k], 16)
                with sp.Fori(1, S // 4) as i:
                    for k in range(4):
                        sp.wait_ge(x_transposed, i * 4 + k - 3)
                        sp.dma_start(x_ring[:, k, :], d["x"][:, bass.ds(i * 4 + k, 1), :]
                                     .rearrange("b o m -> b (o m)")).then_inc(x_loaded[k], 16)

            @block.gpsimd
            def _(pool):
                pool.memset(eps_c[:], LN_EPS).then_inc(consts, 1)
                pool.memset(xT_ring[:], 0.0).then_inc(consts, 1)
                row = lambda name: d[name].rearrange("(o n) -> o n", o=1)
                pool.dma_start(wconv[:].rearrange("p c k -> p (c k)"),
                               d["W_conv"].rearrange("(o c) i k -> o (c i k)", o=1)
                               .to_broadcast([P, DI * TAPS])).then_inc(small_loaded, 16)
                for tile, name, n in ((bconv, "b_conv", DI), (lng, "ln_g", DI), (lnb, "ln_b", DI), (dskip, "D", DI),
                                      (bdt, "b_dt", DS), (alog, "A_log", DS)):
                    pool.dma_start(tile[:], row(name).to_broadcast([P, n])).then_inc(small_loaded, 16)
                pool.dma_start(temb[:], d["cond"]).then_inc(small_loaded, 16)
                with pool.Fori(0, S // NB) as b:
                    pool.wait_ge(scaled_done, b + 1)
                    x_b = xn[:, bass.ds(b * NB, NB), :]
                    pool.tensor_tensor(x_b, x_b, lnb[:].unsqueeze(1).to_broadcast([P, NB, DI]), ALU.add)\
                        .then_inc(shifted, 1)

            @block.tensor
            def _(pe):
                pe.wait_ge(w_in_loaded, 6 * 16)
                for r in range(4):
                    last = pe.transpose(ptr[:, r * P:(r + 1) * P], win[:, r, :], ident[:])
                last.then_inc(set_up, 1)
                for f in range(2):
                    pe.transpose(pconv[:, f * P:(f + 1) * P], wout[:, f * P:(f + 1) * P], ident[:])
                    last = pe.transpose(pconv[:, 256 + f * NPROJ:256 + (f + 1) * NPROJ], wx[:, f * P:(f + 1) * P],
                                        ident[0:NPROJ, 0:NPROJ])
                last.then_inc(set_up, 1)
                for f in range(2):
                    last = pe.matmul(pgate[:, f * DS:(f + 1) * DS], wxdt[:, f * P:(f + 1) * P], wdtT[:],
                                     start=True, stop=True)
                last.then_inc(set_up, 1)
                pe.wait_ge(set_up_used, 4)
                pe.wait_ge(taps_ready, TAPS)

                def transpose_x(t, k):
                    if isinstance(t, int) and t >= S:
                        return
                    pe.wait_ge(x_loaded[k], (t // 4 + 1) * 16)
                    wait_for(pe, xT_ready, t)
                    pe.transpose(ptr[:, 0:P], x_ring[:, k, :], ident[:]).then_inc(x_transposed, 1)

                def step(t, k, more):
                    pe.wait_ge(xT_ready, t + 1)
                    wait_for(pe, pre_ready, t)
                    for tap in range(TAPS):
                        one = pe.matmul(pconv[:, 0:DI], xT_ring[:, (k + 1 + tap) % 4, :], wtap[:, tap, :],
                                        start=(tap == 0), stop=(tap == TAPS - 1))
                        if tap == 0:
                            one.then_inc(oldest_read, 1)
                    one.then_inc(conv_done, 1)
                    if more:
                        transpose_x(t + 1, (k + 1) % 4)
                    wait_for(pe, gate_ready, t)
                    pe.matmul(pgate[:, 0:DI], xT_ring[:, k, :], winT[:, 2:4, :], start=True, stop=True)\
                        .then_inc(gate_done, 1)

                transpose_x(0, 0)
                for t in range(4):
                    step(t, t, True)
                with pe.Fori(1, S // 4 - 1) as i:
                    for k in range(4):
                        step(i * 4 + k, k, True)
                for t in range(S - 4, S):
                    step(t, t % 4, t + 1 < S)

            @block.scalar
            def _(act):
                act.wait_ge(set_up, 1)
                act.copy(winT[:].rearrange("m r p -> m (r p)"), ptr[:]).then_inc(set_up_used, 1)
                act.wait_ge(set_up, 2)
                act.copy(woutT[:].rearrange("p f m -> p (f m)"), pconv[:, 0:2 * P]).then_inc(set_up_used, 1)
                act.copy(proj_w[:, :, 0:2 * DS],
                         pconv[:, 256:256 + 2 * NPROJ].rearrange("p (f n) -> p f n", f=2)[:, :, 0:2 * DS])\
                    .then_inc(set_up_used, 1)
                act.wait_ge(set_up, 3)
                act.copy(proj_w[:, :, 2 * DS:NPROJ], pgate[:, 0:2 * DS].rearrange("p (f n) -> p f n", f=2))\
                    .then_inc(set_up_used, 1)

                def xT_copy(t, k):
                    act.wait_ge(x_transposed, t + 1)
                    wait_for(act, oldest_read, t)
                    if not isinstance(t, int) or t >= 4:
                        wait_for(act, gate_done, t - 3)
                    act.copy(xT_ring[:, k, :], ptr[:, 0:P]).then_inc(xT_ready, 1)

                def step(t, k, more):
                    if more:
                        xT_copy(t + 1, (k + 1) % 4)
                    act.wait_ge(pre_ready, t + 1)
                    act.activation(xn[:, bass.ds(t, 1), :].rearrange("p o c -> p (o c)"), pre[:, k % 2, :], ACT.Silu)\
                        .then_inc(silu_done, 1)
                    act.wait_ge(gate_done, t + 1)
                    act.activation(gate[:, bass.ds(t, 1), :].rearrange("p o c -> p (o c)"), pgate[:, 0:DI], ACT.Silu)\
                        .then_inc(gate_ready, 1)

                act.wait_ge(consts, 2)
                xT_copy(0, 0)
                for t in range(4):
                    step(t, t, True)
                with act.Fori(1, S // 4 - 1) as i:
                    for k in range(4):
                        step(i * 4 + k, k, True)
                for t in range(S - 4, S):
                    step(t, t % 4, t + 1 < S)
                act.preload_act_table_set(EXP_LN)
                act.wait_ge(mv_done, S)
                act.activation(ln_tmp[:], mv[:, :, 1], ACT.Ln, bias=eps_c[:]).then_inc(ln_done, 1)
                act.wait_ge(ln_done, 1)
                act.activation(rstd[:], ln_tmp[:], ACT.Exp, scale=-0.5).then_inc(rstd_ready, 1)

                def square(b, k):
                    act.wait_ge(shifted, b + 1)
                    wait_for(act, sums_done, b - 1)
                    act.activation(sqs[:, k, :, :], xn[:, bass.ds(b * NB, NB), :], ACT.Square).then_inc(sq_done, 1)

                square(0, 0)
                square(1, 1)
                with act.Fori(1, S // NB // 2) as i:
                    for k in range(2):
                        square(i * 2 + k, k)
                act.wait_ge(norm_clamped, 1)
                act.activation(ln_tmp[:], nrm[:], ACT.Ln).then_inc(ln_done, 1)
                act.wait_ge(ln_done, 2)
                act.activation(nrm[:], ln_tmp[:], ACT.Exp, scale=0.5).then_inc(nrm_ready, 1)
                act.activation(neg_a[:], alog[:], ACT.Tanh).then_inc(nrm_ready, 1)

            @block.vector
            def _(dve):
                dve.wait_ge(small_loaded, 8 * 16)
                dve.wait_ge(set_up_used, 1)
                for k in range(TAPS):
                    dve.tensor_tensor(wtap[:, k, :], winT[:, 0:2, :].rearrange("m r p -> m (r p)"), wconv[:, :, k],
                                      ALU.mult).then_inc(taps_ready, 1)
                done = 0
                for t in range(TAPS):
                    dve.tensor_tensor(tap_tmp[:], temb[:], wconv[:, :, TAPS - 1 - t], ALU.mult).then_inc(chain, 1)
                    done += 1
                    dve.wait_ge(chain, done)
                    dve.tensor_tensor(tap_bias[:, t, :], tap_tmp[:], bconv[:] if t == 0 else tap_bias[:, t - 1, :],
                                      ALU.add).then_inc(chain, 1)
                    done += 1
                    dve.wait_ge(chain, done)

                def statistics(t, k):
                    dve.wait_ge(silu_done, t + 1)
                    wait_for(dve, aggr_done, t - 1)
                    dve.bn_stats(stats[:, k % 2, :], xn[:, bass.ds(t, 1), :].rearrange("p o c -> p (o c)"))\
                        .then_inc(stats_done, 1)
                    dve.wait_ge(stats_done, t + 1)
                    if not isinstance(t, int) or t:
                        keep(t - 1, k - 1)
                    dve.bn_aggr(mv_t[:, k % 2, :], stats[:, k % 2, :]).then_inc(aggr_done, 1)

                def keep(t, k):
                    dve.wait_ge(aggr_done, t + 1)
                    dve.tensor_copy(mv[:, bass.ds(t, 1), :].rearrange("p o c -> p (o c)"), mv_t[:, k % 2, :])\
                        .then_inc(mv_done, 1)

                def step(t, k):
                    dve.wait_ge(conv_done, t + 1)
                    wait_for(dve, silu_done, t - 1)
                    bias = tap_bias[:, min(t, TAPS - 1) if isinstance(t, int) else TAPS - 1, :]
                    dve.tensor_tensor(pre[:, k % 2, :], pconv[:, 0:DI], bias, ALU.add).then_inc(pre_ready, 1)

                for t in range(4):
                    step(t, t)
                    if t:
                        statistics(t - 1, t - 1)
                with dve.Fori(1, S // 4) as i:
                    for k in range(4):
                        step(i * 4 + k, k)
                        statistics(i * 4 + k - 1, (k - 1) % 4)
                statistics(S - 1, (S - 1) % 4)
                keep(S - 1, (S - 1) % 4)
                dve.wait_ge(rstd_ready, 1)

                def scaled(b):
                    for q in range(NB):
                        t = b * NB + q
                        x_t = xn[:, bass.ds(t, 1), :].rearrange("p o c -> p (o c)")
                        dve.tensor_scalar(x_t, x_t, mv[:, bass.ds(t, 1), 0], rstd[:, bass.ds(t, 1)],
                                          ALU.subtract, ALU.mult).then_inc(centred, 1)
                    dve.wait_ge(centred, NB * b + NB)
                    x_b = xn[:, bass.ds(b * NB, NB), :]
                    dve.tensor_tensor(x_b, x_b, lng[:].unsqueeze(1).to_broadcast([P, NB, DI]), ALU.mult)\
                        .then_inc(scaled_done, 1)

                def summed(b, k):
                    dve.wait_ge(sq_done, b + 1)
                    dve.reduce_sum(nrm[:, bass.ds(b * NB, NB)], sqs[:, k, :, :], AX.X).then_inc(sums_done, 1)

                scaled(0)
                scaled(1)
                with dve.Fori(1, S // NB // 2) as i:
                    for k in range(2):
                        scaled(i * 2 + k)
                        summed(i * 2 + k - 2, k)
                for k in range(2):
                    summed(S // NB - 2 + k, k)
                dve.wait_ge(sums_done, S // NB)
                dve.tensor_scalar(nrm[:], nrm[:], 1e-19, 1.0, ALU.max, ALU.min).then_inc(norm_clamped, 1)
                dve.wait_ge(nrm_ready, 2)
                dve.tensor_scalar(neg_a[:], neg_a[:], -0.01, None, ALU.mult).then_inc(chain, 1)

        scan_phase(nc, ctx, sb, sem, pb, dict(ident=ident, xn=xn, gate=gate, nrm=nrm, neg_a=neg_a, proj_w=proj_w,
                                              woutT=woutT, bdt=bdt, dskip=dskip, ptr=ptr, pproj=pgate, res=res, u=u))


def scan_phase(nc, ctx, sb, sem, pb, a):
    ident, xn, gate, nrm, neg_a = a["ident"], a["xn"], a["gate"], a["nrm"], a["neg_a"]
    proj_w, woutT, bdt, dskip, ptr, pproj, res, u = (a[k] for k in "proj_w woutT bdt dskip ptr pproj res u".split())
    NS = DS * DI
    x_now = sb("s_x", [P, 2, DI])
    xnT = sb("s_xnT", [P, 2, P])
    decay = sb("s_decay", [P, 2, DS])
    bd = sb("s_bd", [P, 2, DS])
    cm = sb("s_cm", [P, 2, DS])
    dtp = sb("s_dtp", [P, DS])
    dtt = sb("s_dtt", [P, DS])
    h = sb("s_h", [P, 2, DS, DI])
    cdiag = sb("s_cdiag", [P, 2, DS, P])
    dx = sb("s_dx", [P, 2, DI])
    z = sb("s_z", [P, 2, DI])
    zT = sb("s_zT", [P, 2, P])
    py = [pb(f"s_py{k}", [P, 512]) for k in range(2)]
    pout = pb("s_pout", [P, 512])
    pzT = pb("s_pzT", [P, 512])

    x_copied, xT_done, xT_copied = sem("s_x_copied"), sem("s_xT_done"), sem("s_xT_copied")
    proj_done, proj_read, dt_pre, dt_tanh, decay_ready = (sem(n) for n in (
        "s_proj_done", "s_proj_read", "s_dt_pre", "s_dt_tanh", "s_decay_ready"))
    u_ready, h_cell, h_ready = sem("s_u_ready"), sem("s_h_cell"), sem("s_h_ready")
    side_mul, side_ready = sem("s_side_mul"), sem("s_side_ready")
    cdiag_ready, dx_ready, y_done, z_sum, z_ready = (sem(n) for n in (
        "s_cdiag_ready", "s_dx_ready", "s_y_done", "s_z_sum", "s_z_ready"))
    zT_done, zT_copied, out_done, res_written, zeroed = (sem(n) for n in (
        "s_zT_done", "s_zT_copied", "s_out_done", "s_res_written", "s_zeroed"))
    at = lambda buf, t: buf[:, bass.ds(t, 1), :].rearrange("p o c -> p (o c)")
    live = lambda t: not isinstance(t, int) or 0 <= t < S

    def turns(eng, turn):
        for t in range(-2, 4):
            turn(t, t % 2)
        with eng.Fori(2, S // 2 - 1) as i:
            for k in range(2):
                turn(i * 2 + k, k)
        for t in range(S - 2, S + 2):
            turn(t, t % 2)

    with nc.Block() as block:
        @block.tensor
        def _(pe):
            def transpose_x(t, k):
                pe.wait_ge(x_copied, t + 1)
                wait_for(pe, xT_copied, t)
                for f in range(2):
                    last = pe.transpose(ptr[:, f * P:(f + 1) * P], x_now[:, k, f * P:(f + 1) * P], ident[:])
                last.then_inc(xT_done, 1)

            def project(t):
                pe.wait_ge(xT_copied, t + 1)
                wait_for(pe, proj_read, 2 * t)
                wait_for(pe, dt_pre, t)
                for f in range(2):
                    last = pe.matmul(pproj[:, 0:NPROJ], xnT[:, f, :], proj_w[:, f, :], start=(f == 0), stop=(f == 1))
                last.then_inc(proj_done, 1)

            def y_product(t, k):
                pe.wait_ge(cdiag_ready, t + 1)
                pe.wait_ge(h_ready, t + 1)
                wait_for(pe, z_sum, t - 1)
                for s in range(DS):
                    last = pe.matmul(py[k][:, 0:DI], cdiag[:, k, s, :], h[:, k, s, :], start=(s == 0),
                                     stop=(s == DS - 1))
                last.then_inc(y_done, 1)

            def transpose_z(t, k):
                pe.wait_ge(z_ready, t + 1)
                wait_for(pe, zT_copied, t)
                for f in range(2):
                    last = pe.transpose(pzT[:, f * P:(f + 1) * P], z[:, k, f * P:(f + 1) * P], ident[:])
                last.then_inc(zT_done, 1)

            def output(t):
                pe.wait_ge(zT_copied, t + 1)
                wait_for(pe, res_written, t)
                for f in range(2):
                    last = pe.matmul(pout[:, 0:P], woutT[:, f, :], zT[:, f, :], start=(f == 0), stop=(f == 1))
                last.then_inc(out_done, 1)

            def turn(t, k):
                if live(t + 2):
                    transpose_x(t + 2, k)
                if live(t - 2):
                    transpose_z(t - 2, k)
                if live(t + 2):
                    project(t + 2)
                if live(t - 2):
                    output(t - 2)
                if live(t):
                    y_product(t, k)

            turns(pe, turn)

        @block.scalar
        def _(act):
            def outer(t, k):
                act.wait_ge(proj_read, 2 * t + 1)
                act.wait_ge(x_copied, t + 1)
                wait_for(act, h_cell, (DS - PS) * (t - 1))
                wait_for(act, side_ready, t - 1)
                for s in range(DS):
                    act.activation(u[:, k, s, :], x_now[:, k, :], ACT.Copy, scale=bd[:, k, s:s + 1])\
                        .then_inc(u_ready, 1)

            def turn(t, k):
                if live(t + 1):
                    outer(t + 1, 1 - k)
                if live(t + 2):
                    act.wait_ge(xT_done, t + 3)
                    act.copy(xnT[:].rearrange("p f b -> p (f b)"), ptr[:, 0:2 * P]).then_inc(xT_copied, 1)
                if live(t - 2):
                    act.wait_ge(zT_done, t - 1)
                    act.copy(zT[:].rearrange("p f b -> p (f b)"), pzT[:, 0:2 * P]).then_inc(zT_copied, 1)
                    act.wait_ge(out_done, t - 1)
                    act.copy(res[:].rearrange("p (b t) -> p b t", t=S)[:, :, bass.ds(t - 2, 1)],
                             pout[:, 0:P].rearrange("p (b o) -> p b o", o=1)).then_inc(res_written, 1)
                if live(t + 2):
                    act.wait_ge(dt_pre, t + 3)
                    wait_for(act, decay_ready, 2 * (t + 1) + 1)
                    act.activation(dtt[:], dtp[:], ACT.Tanh).then_inc(dt_tanh, 1)

            turns(act, turn)

        @block.gpsimd
        def _(pool):
            def turn(t, k):
                if live(t):
                    pool.wait_ge(decay_ready, 2 * t + 2)
                    if isinstance(t, int) and t == 0:
                        pool.wait_ge(zeroed, 1)
                    wait_for(pool, h_ready, t)
                    wait_for(pool, y_done, t - 1)
                    side = h[:, k, 0:PS, :]
                    pool.tensor_tensor(side, h[:, 1 - k, 0:PS, :], decay[:, k, 0:PS].unsqueeze(2)
                                       .to_broadcast([P, PS, DI]), ALU.mult).then_inc(side_mul, 1)
                    pool.wait_ge(side_mul, t + 1)
                    pool.wait_ge(u_ready, DS * t + PS)
                    pool.tensor_tensor(side, side, u[:, k, 0:PS, :], ALU.add).then_inc(side_ready, 1)
                if live(t):
                    wait_for(pool, z_sum, t - 1)
                    pool.wait_ge(x_copied, t + 1)
                    pool.tensor_tensor(dx[:, k, :], x_now[:, k, :], dskip[:], ALU.mult).then_inc(dx_ready, 1)
                if live(t + 2):
                    wait_for(pool, u_ready, DS * (t + 1))
                    wait_for(pool, xT_done, t + 1)
                    wait_for(pool, dx_ready, t + 1)
                    pool.tensor_copy(x_now[:, k, :], at(xn, t + 2)).then_inc(x_copied, 1)
                if live(t + 1):
                    pool.wait_ge(proj_read, 2 * (t + 1) + 2)
                    wait_for(pool, y_done, t)
                    pool.tensor_tensor(cdiag[:, 1 - k, :, :], ident[:].unsqueeze(1).to_broadcast([P, DS, P]),
                                       cm[:, 1 - k, :].unsqueeze(2).to_broadcast([P, DS, P]), ALU.mult)\
                        .then_inc(cdiag_ready, 1)

            turns(pool, turn)

        @block.vector
        def _(dve):
            def project(t, k):
                dve.wait_ge(proj_done, t + 1)
                wait_for(dve, u_ready, DS * (t - 1))
                dve.tensor_scalar(bd[:, k, :], pproj[:, 0:DS], nrm[:, bass.ds(t, 1)], None, ALU.mult)\
                    .then_inc(proj_read, 1)
                wait_for(dve, cdiag_ready, t - 1)
                dve.tensor_copy(cm[:, k, :], pproj[:, DS:2 * DS]).then_inc(proj_read, 1)
                wait_for(dve, dt_tanh, t)
                dve.tensor_tensor(dtp[:], pproj[:, 2 * DS:NPROJ], bdt[:], ALU.add).then_inc(dt_pre, 1)

            def set_decay(t, k):
                dve.wait_ge(dt_tanh, t + 1)
                dve.tensor_tensor(decay[:, k, :], dtt[:], neg_a[:], ALU.mult).then_inc(decay_ready, 1)
                dve.wait_ge(decay_ready, 2 * t + 1)
                dve.tensor_scalar(decay[:, k, :], decay[:, k, :], 1.0, None, ALU.add).then_inc(decay_ready, 1)

            def scan(t, k):
                dve.wait_ge(decay_ready, 2 * t + 2)
                wait_for(dve, h_ready, t)
                wait_for(dve, y_done, t - 1)
                for s in range(PS, DS):
                    dve.wait_ge(u_ready, DS * t + s + 1)
                    dve.scalar_tensor_tensor(h[:, k, s, :], h[:, 1 - k, s, :], decay[:, k, s:s + 1], u[:, k, s, :],
                                             ALU.mult, ALU.add).then_inc(h_cell, 1)
                dve.wait_ge(h_cell, (DS - PS) * (t + 1))
                dve.wait_ge(side_ready, t + 1)
                flat = h[:, k, :, :].rearrange("p s c -> p (s c)")
                dve.tensor_scalar(flat, flat, 10.0, -10.0, ALU.min, ALU.max).then_inc(h_ready, 1)

            def gated(t, k):
                dve.wait_ge(y_done, t + 1)
                dve.wait_ge(dx_ready, t + 1)
                wait_for(dve, zT_done, t - 1)
                dve.tensor_tensor(z[:, k, :], py[k][:, 0:DI], dx[:, k, :], ALU.add).then_inc(z_sum, 1)
                dve.wait_ge(z_sum, t + 1)
                dve.tensor_tensor(z[:, k, :], z[:, k, :], at(gate, t), ALU.mult).then_inc(z_ready, 1)

            def turn(t, k):
                if live(t):
                    scan(t, k)
                if live(t + 1):
                    set_decay(t + 1, 1 - k)
                if live(t + 2):
                    project(t + 2, k)
                if live(t - 1):
                    gated(t - 1, 1 - k)

            dve.memset(h[:, 1, :, :], 0.0).then_inc(zeroed, 1)
            dve.wait_ge(zeroed, 1)
            turns(dve, turn)


def stack(nc, d, res):
    with ExitStack() as ctx:
        def sb(name, shape, dt=F32):
            return ctx.enter_context(nc.sbuf_tensor(name, shape, dt))

        def pb(name, shape):
            return ctx.enter_context(nc.psum_tensor(name, shape, F32))

        def sem(name):
            return ctx.enter_context(nc.semaphore(name))

        ident = sb("ident_sb", [P, P])
        ident_b = sb("ident_b", [P, P], BF16)
        center = sb("center_sb", [P, P])
        mean = sb("mean_sb", [P, P])
        mask_f = sb("mask_f", [P, HEADS * S])
        mask_b = sb("mask_b", [P, HEADS * S], BF16)
        rot_const = sb("rot_const", [P, 4, DH])
        eps_c = sb("eps_c", [P, 1])
        norm_c = sb("norm_c", [P, 1])

        w_raw = sb("w_raw", [DM, 3 * INNER])
        w_hi = sb("w_hi", [DM, 3 * INNER], F32R)
        w_lo = sb("w_lo", [DM, 3 * INNER], F32R)
        wo = sb("wo", [P, HP, DM])
        w1 = sb("w1", [DM, 2 * HID])
        w2 = sb("w2", [P, 3, DM])
        b1 = sb("b1", [P, 2, 3])
        ln_par = sb("ln_par", [DM, 3])
        qk_scale = sb("qk_scale", [P, 2, DH])
        rot = sb("rot", [P, 4, DH])

        xs_hi = sb("xs_hi", [DM, 2, P], F32R)
        xs_lo = sb("xs_lo", [DM, 2, P], F32R)
        sq = sb("sq", [P, INNER])
        ss = sb("ss", [P, 2, HEADS])
        ln_ss = sb("ln_ss", [P, 2, HEADS])
        qk_n = sb("qk_n", [P, 2, INNER])
        qk_r = sb("qk_r", [P, 2, INNER])
        qk_t = sb("qk_t", [P, 2, INNER])
        qT = sb("qT", [P, HP, P])
        kT = sb("kT", [P, HP, TILE_B, 2, S])
        v = sb("v", [P, GT, INNER])
        top = sb("top", [P, HEADS])
        sm = sb("sm", [P, HEADS * S])
        pr = sb("pr", [P, HEADS * S])
        den = sb("den", [P, HEADS])
        rden = sb("rden", [P, HEADS])
        pT = sb("pT", [P, HEADS, P])
        oT = sb("oT", [P, 2, HP, GT, P])
        fs = sb("fs", [DM, GTOK])
        fc = sb("fc", [DM, GTOK])
        fsq = sb("fsq", [DM, GTOK])
        frs = sb("frs", [DM, GTOK])
        fn = sb("fn", [DM, GTOK])
        gt = sb("gt", [P, 3, GTOK])

        pa = [pb(f"pa{k}", [P, INNER]) for k in range(2)]
        px = pb("px", [P, INNER])
        ps = pb("ps", [P, HEADS * S])
        pg = pb("pg", [P, GTOK])

        names = """const_loaded mask_ready zeroed wqkv_loaded wo_loaded ffn_loaded
            qk_scale_loaded rot_ready w_hi_ready w_lo_ready xs_hi_ready xs_ready q_full k_full v_full
            sq_q sq_k sum_q sum_k clamp_q clamp_k ln_q ln_k inv_q inv_k
            norm_q norm_k cos_q cos_k sin_q sin_k rot_q rot_k tq_done tq_out tk_done tk_out v_out
            scores_done top_done sub_done exp_done den_done rden_done probs_done pT_done pv_done pv_out
            wo_done res_attn fs_ready center_done fc_ready fsq_ready var_done fln_done frs_ready fn_mul fn_ready
            gate_done gate_out gelu_done a_done h_ready w2_done res_ready""".split()
        s = {n: sem(n) for n in names}

        heads = lambda ap: ap.rearrange("p (h e) -> p h e", e=DH)
        halves = lambda ap: ap.rearrange("p (h f e) -> p h f e", f=2, e=DH // 2)
        keys = lambda ap: ap.rearrange("p (h j) -> p h j", j=S)
        over = lambda ap, n: ap.unsqueeze(2).to_broadcast([P, ap.shape[1], n])
        per_head = lambda ap: ap.unsqueeze(1).to_broadcast([P, HEADS, ap.shape[1]])

        def late(copy, dst, src):
            dst = dst.rearrange("p (b t) -> p b t", t=S)
            src = src.rearrange("p (b t) -> p b t", t=S)
            return copy(dst[:, :, 1:S], src[:, :, 0:S - 1])

        def group_steps(eng, body, new_layer):
            new_layer(0)
            body(0)
            body(1)
            with eng.Fori(2, GROUPS) as i:
                body(i)
            with eng.Fori(1, DEPTH) as l:
                new_layer(l)
                with eng.Fori(0, GROUPS) as g:
                    body(l * GROUPS + g)
            body(NG)
            body(NG + 1)

        class Live:
            def __init__(self, i, j):
                k = i if isinstance(i, int) else 2
                n = k * GT + j
                last = NG if isinstance(i, int) else NG + 9
                nt = last * GT
                self.qkv = n < nt
                self.score = 1 <= n <= nt
                self.pv = 2 <= n <= nt + 1
                self.prev = 1 <= k <= last
                self.prev2 = 2 <= k <= last + 1

        with nc.Block() as block:
            @block.sync
            def _(sp):
                for dst, name in ((ident, "ident"), (center, "center"), (mean, "mean"), (mask_f, "mask")):
                    sp.dma_start(dst[:], d[name]).then_inc(s["const_loaded"], 16)
                sp.dma_start(rot_const[:].rearrange("p a e -> p (a e)"), d["rot"]).then_inc(s["const_loaded"], 16)

                def of(name, l):
                    ap = d[name][bass.ds(l, 1)]
                    return ap.rearrange("o a b -> (o a) b") if len(ap.shape) == 3 else ap

                def load_qkv(l):
                    sp.dma_start(w_raw[:], of("Wqkv", l)).then_inc(s["wqkv_loaded"], 16)

                def load_scales(l):
                    for c, name in enumerate(("q_scale", "k_scale")):
                        sp.dma_start(qk_scale[:, c, :], of(name, l).to_broadcast([P, DH]))\
                            .then_inc(s["qk_scale_loaded"], 16)

                def load_wo(l):
                    sp.dma_start(wo[:], of("Wo", l).rearrange("(h p) m -> p h m", p=P)).then_inc(s["wo_loaded"], 16)

                def load_ffn(l):
                    sp.dma_start(w1[:], of("W1", l)).then_inc(s["ffn_loaded"], 16)
                    w2_l, b1_l = of("W2", l), of("b1", l)
                    two = 2 * P
                    sp.dma_start(w2[:, 0:2, :], w2_l[0:two, :].rearrange("(h p) m -> p h m", p=P))\
                        .then_inc(s["ffn_loaded"], 16)
                    sp.dma_start(w2[0:HID - two, 2, :], w2_l[two:HID, :]).then_inc(s["ffn_loaded"], 16)
                    for c in range(2):
                        at = c * HID
                        sp.dma_start(b1[:, c, 0:2], b1_l[:, at:at + two].rearrange("o (h p) -> p (o h)", p=P))\
                            .then_inc(s["ffn_loaded"], 16)
                        sp.dma_start(b1[0:HID - two, c, 2:3], b1_l[:, at + two:at + HID].rearrange("o p -> p o"))\
                            .then_inc(s["ffn_loaded"], 16)
                    for c, name in enumerate(("ffn_ln_g", "ffn_ln_b", "b2")):
                        sp.dma_start(ln_par[:, c:c + 1], of(name, l).rearrange("o p -> p o"))\
                            .then_inc(s["ffn_loaded"], 16)

                load_qkv(0)
                load_scales(0)
                load_wo(0)
                load_ffn(0)

                def next_layer(l):
                    sp.wait_ge(s["wo_done"], l * GROUPS)
                    load_wo(l)
                    sp.wait_ge(s["res_ready"], l * GROUPS + GROUPS)
                    load_ffn(l)

                with sp.Fori(1, DEPTH) as l:
                    sp.wait_ge(s["w_lo_ready"], 3 * l)
                    load_qkv(l)
                    sp.wait_ge(s["rot_ready"], ROT_OPS * l)
                    load_scales(l)
                    next_layer(l)

            @block.tensor
            def _(pe):
                def qkv(i, j):
                    n = i * GT + j
                    l, u = i // GROUPS, 3 * j
                    pe.wait_ge(s["xs_ready"], 2 * (n + 1))
                    for c, full, free in ((0, "q_full", ("norm_k", n)), (1, "k_full", ("v_out", n)),
                                          (2, "v_full", ("norm_q", n + 1))):
                        wait_for(pe, s[free[0]], free[1])
                        if j == 0:
                            pe.wait_ge(s["w_lo_ready"], 3 * l + c + 1)
                        for half in range(2):
                            at = slice(c * INNER + half * 512, c * INNER + half * 512 + 512)
                            for k, (x, w) in enumerate(((xs_hi, w_hi), (xs_hi, w_lo), (xs_lo, w_hi))):
                                last = pe.matmul(pa[(u + c) % 2][:, half * 512:half * 512 + 512], x[:, j % 2, :],
                                                 w[:, at], start=(k == 0), stop=(k == 2))
                        last.then_inc(s[full], 1)
                        yield

                def transposes(n, c, ready, free, done):
                    pe.wait_ge(s[ready], n + 1)
                    wait_for(pe, s[free[0]], free[1])
                    for hp in range(HP):
                        last = pe.transpose(px[:, hp * P:(hp + 1) * P], qk_r[:, c, hp * P:(hp + 1) * P], ident[:])
                    last.then_inc(s[done], 1)

                def scores(n):
                    pe.wait_ge(s["tq_out"], n + 1)
                    wait_for(pe, s["sub_done"], n)
                    pe.matmul(ps[:], ident_b[:], mask_b[:], start=True, stop=False, skip_group_check=True)
                    pe.wait_ge(s["tk_out"], 2 * (n + 1))
                    for b in range(TILE_B):
                        rows = slice(b * S, (b + 1) * S)
                        for hp in range(HP):
                            last = pe.matmul(ps[rows, hp * 2 * S:(hp + 1) * 2 * S], qT[:, hp, rows],
                                             kT[:, hp, b, :, :].rearrange("p h j -> p (h j)"), start=False, stop=True,
                                             skip_group_check=True)
                    last.then_inc(s["scores_done"], 1)

                def weigh_values(n, j, scored):
                    pe.wait_ge(s["pT_done"], TILE_B * (n + 1))
                    pe.wait_ge(s["v_out"], n + 1)
                    if scored:
                        pe.wait_ge(s["tk_out"], 2 * (n + 2))
                    else:
                        pe.wait_ge(s["pv_out"], n)
                    for h in range(HEADS):
                        at = (h % 2) * DH
                        last = pe.matmul(px[at:at + DH, (h // 2) * P:(h // 2 + 1) * P],
                                         v[:, (j - 2) % GT, h * DH:(h + 1) * DH], pT[:, h, :], start=True, stop=True,
                                         skip_group_check=True)
                    last.then_inc(s["pv_done"], 1)

                def project_out(g, lo, hi):
                    if lo == 0:
                        pe.wait_ge(s["pv_out"], GT * (g + 1))
                        pe.wait_ge(s["wo_loaded"], (g // GROUPS + 1) * 16)
                        wait_for(pe, s["res_ready"], g + GROUPS)
                    for hp in range(lo, hi):
                        heads_out = oT[:, bass.ds(g % 2, 1), hp, :, :].rearrange("p o t n -> p (o t n)")
                        last = pe.matmul(pg[:], wo[:, hp, :], heads_out,
                                         start=(hp == 0), stop=(hp == HP - 1))
                    if hi == HP:
                        last.then_inc(s["wo_done"], 1)

                def subtract_mean(g):
                    pe.wait_ge(s["fs_ready"], 2 * (g + 1))
                    pe.wait_ge(s["res_attn"], g + 1)
                    pe.matmul(pg[:], center[:], fs[:], start=True, stop=True).then_inc(s["center_done"], 1)

                def variance(g):
                    pe.wait_ge(s["fsq_ready"], g + 1)
                    pe.matmul(pg[:], mean[:], fsq[:], start=True, stop=True).then_inc(s["var_done"], 1)

                def gate_block(g, k):
                    if k == 0:
                        pe.wait_ge(s["fn_ready"], g + 1)
                        pe.wait_ge(s["ffn_loaded"], (g // GROUPS + 1) * FFN_DMAS * 16)
                    else:
                        pe.wait_ge(s["gate_out"], 3 * g + k)
                    at, m = HBLK[k]
                    pe.matmul(pg[0:m, :], w1[:, HID + at:HID + at + m], fn[:], start=True, stop=True)\
                        .then_inc(s["gate_done"], 1)

                def a_block(g, k):
                    if k == 0:
                        pe.wait_ge(s["gate_out"], 3 * g + 3)
                    else:
                        pe.wait_ge(s["h_ready"], 3 * g + k)
                    at, m = HBLK[k]
                    pe.matmul(pg[0:m, :], w1[:, at:at + m], fn[:], start=True, stop=True).then_inc(s["a_done"], 1)

                def down(g):
                    pe.wait_ge(s["h_ready"], 3 * g + 3)
                    for k, (at, m) in enumerate(HBLK):
                        last = pe.matmul(pg[:], w2[0:m, k, :], gt[0:m, k, :], start=(k == 0), stop=(k == 2))
                    last.then_inc(s["w2_done"], 1)

                def body(i):
                    for j in range(GT):
                        n, live = i * GT + j, Live(i, j)
                        part = qkv(i, j) if live.qkv else iter(())
                        new, old = live.prev, live.prev2
                        extra = {
                            0: [old and (lambda: subtract_mean(i - 2)),
                                old and (lambda: variance(i - 2)),
                                old and (lambda: gate_block(i - 2, 0)),
                                None,
                                None],
                            1: [old and (lambda: gate_block(i - 2, 1)),
                                old and (lambda: gate_block(i - 2, 2)),
                                None,
                                old and (lambda: a_block(i - 2, 0)),
                                None],
                            2: [None,
                                old and (lambda: a_block(i - 2, 1)),
                                old and (lambda: a_block(i - 2, 2)),
                                None,
                                old and (lambda: down(i - 2))],
                            3: [None,
                                new and (lambda: project_out(i - 1, 0, HP // 2)),
                                new and (lambda: project_out(i - 1, HP // 2, HP)),
                                None,
                                None],
                        }[j]
                        slot = lambda k: extra[k]() if extra[k] else None
                        next(part, None)
                        slot(0)
                        if live.score:
                            transposes(n - 1, 0, "rot_q", ("pv_out", n - 2), "tq_done")
                        slot(1)
                        next(part, None)
                        if live.score:
                            transposes(n - 1, 1, "rot_k", ("tq_out", n), "tk_done")
                        slot(2)
                        next(part, None)
                        if live.score:
                            scores(n - 1)
                        slot(3)
                        if live.pv:
                            weigh_values(n - 2, j, live.score)
                        slot(4)

                pe.wait_ge(s["const_loaded"], 5 * 16)
                pe.wait_ge(s["mask_ready"], 2)
                pe.wait_ge(s["zeroed"], 8)
                group_steps(pe, body, lambda l: None)

            @block.scalar
            def _(act):
                def square(c, k, full, n, sq_sem, sum_sem):
                    act.wait_ge(s[full], n + 1)
                    wait_for(act, s[sum_sem[0]], n + sum_sem[1])
                    act.activation(sq[:], pa[k][:], ACT.Square).then_inc(s[sq_sem], 1)

                def inverse_norm(c, n, clamp, ln, inv):
                    act.wait_ge(s[clamp], n + 1)
                    act.activation(ln_ss[:, c, :], ss[:, c, :], ACT.Ln).then_inc(s[ln], 1)
                    act.wait_ge(s[ln], n + 1)
                    act.activation(ss[:, c, :], ln_ss[:, c, :], ACT.Exp, scale=-0.5, bias=norm_c[:])\
                        .then_inc(s[inv], 1)

                def gate_bias(g, k):
                    m = HBLK[k][1]
                    act.wait_ge(s["gate_done"], 3 * g + k + 1)
                    act.activation(gt[0:m, k, :], pg[0:m, :], ACT.Identity, bias=b1[0:m, 1, k:k + 1])\
                        .then_inc(s["gate_out"], 1)

                def shift_hi(n, k):
                    at = bass.ds((n % TILES) * P, P)
                    act.wait_ge(s["res_ready"], n // GT + 1)
                    if not isinstance(n, int) or n >= 2:
                        act.wait_ge(s["v_full"], n - 1)
                    act.copy(xs_hi[0:64, k, :], res[0:64, at]).then_inc(s["xs_hi_ready"], 1)
                    late(act.copy, xs_hi[64:P, k, :], res[64:P, at]).then_inc(s["xs_hi_ready"], 1)

                def new_layer(l):
                    act.wait_ge(s["wqkv_loaded"], 16 * (l + 1))
                    if not isinstance(l, int):
                        act.wait_ge(s["v_full"], l * TILES)
                    for c in range(3):
                        at = slice(c * INNER, (c + 1) * INNER)
                        act.copy(w_hi[:, at], w_raw[:, at]).then_inc(s["w_hi_ready"], 1)

                def body(i):
                    for j in range(GT):
                        n, live = i * GT + j, Live(i, j)
                        u = 3 * j
                        if live.qkv:
                            square(0, u % 2, "q_full", n, "sq_q", ("sum_k", 0))
                        if live.prev2 and j == 1:
                            gate_bias(i - 2, 1)
                        if live.prev2 and j == 0:
                            act.wait_ge(s["center_done"], i - 1)
                            act.copy(fc[:], pg[:]).then_inc(s["fc_ready"], 1)
                            act.wait_ge(s["fc_ready"], i - 1)
                            act.activation(fsq[:], fc[:], ACT.Square).then_inc(s["fsq_ready"], 1)
                        if live.score:
                            act.wait_ge(s["tq_done"], n)
                            act.copy(qT[:].rearrange("p h n -> p (h n)"), px[:]).then_inc(s["tq_out"], 1)
                        if live.qkv:
                            inverse_norm(0, n, "clamp_q", "ln_q", "inv_q")
                        if live.prev2 and j == 0:
                            act.wait_ge(s["var_done"], i - 1)
                            act.activation(frs[:], pg[:], ACT.Ln, bias=eps_c[:]).then_inc(s["fln_done"], 1)
                            act.wait_ge(s["fln_done"], i - 1)
                            act.activation(frs[:], frs[:], ACT.Exp, scale=-0.5).then_inc(s["frs_ready"], 1)
                        if live.prev2 and j == 1:
                            gate_bias(i - 2, 2)
                        if live.qkv:
                            square(1, (u + 1) % 2, "k_full", n, "sq_k", ("sum_q", 1))
                        if live.score:
                            act.wait_ge(s["tk_done"], n)
                            for half in range(2):
                                rows = slice(half * DH, (half + 1) * DH)
                                act.copy(kT[rows, :, :, half, :].rearrange("p h b j -> p (h b) j"),
                                         px[rows, :].rearrange("p (h j) -> p h j", j=S)).then_inc(s["tk_out"], 1)
                        if live.qkv:
                            inverse_norm(1, n, "clamp_k", "ln_k", "inv_k")
                            if not isinstance(n, int) or n + 1 < NT:
                                shift_hi(n + 1, (j + 1) % 2)
                        if live.prev2 and j == 0:
                            gate_bias(i - 2, 0)
                        if live.prev2 and j == 1:
                            act.wait_ge(s["gate_out"], 3 * (i - 1))
                            act.activation(gt[:], gt[:], ACT.Gelu).then_inc(s["gelu_done"], 1)
                            act.preload_act_table_set(EXP_LN)
                        if live.qkv:
                            act.wait_ge(s["v_full"], n + 1)
                            act.copy(v[:, j, :], pa[(u + 2) % 2][:]).then_inc(s["v_out"], 1)
                        if live.prev and j == 3:
                            at = (i - 1) % GROUPS * GTOK
                            act.wait_ge(s["res_attn"], i)
                            act.copy(fs[0:64, :], res[0:64, bass.ds(at, GTOK)]).then_inc(s["fs_ready"], 1)
                            late(act.copy, fs[64:P, :], res[64:P, bass.ds(at, GTOK)]).then_inc(s["fs_ready"], 1)
                        if live.score:
                            act.wait_ge(s["sub_done"], n)
                            act.activation(pr[:], sm[:], ACT.Exp, scale=QK_SCALE).then_inc(s["exp_done"], 1)
                        if live.pv:
                            g = i if j >= 2 else i - 1
                            act.wait_ge(s["pv_done"], n - 1)
                            if j == 2 and (not isinstance(g, int) or g >= 2):
                                act.wait_ge(s["wo_done"], g - 1)
                            act.copy(oT[:, bass.ds(g % 2, 1), :, (j - 2) % GT, :].rearrange("p o h n -> p (o h) n"),
                                     px[:].rearrange("p (h n) -> p h n", n=P)).then_inc(s["pv_out"], 1)

                act.preload_act_table_set(EXP_LN)
                act.wait_ge(s["zeroed"], 8)
                shift_hi(0, 0)
                group_steps(act, body, new_layer)

            @block.vector
            def _(dve):
                def sum_squares(c, n, sq_sem, sum_sem, clamp, inv):
                    dve.wait_ge(s[sq_sem], n + 1)
                    wait_for(dve, s[inv], n)
                    dve.reduce_sum(ss[:, c, :], heads(sq[:]), AX.X).then_inc(s[sum_sem], 1)
                    dve.wait_ge(s[sum_sem], n + 1)
                    dve.tensor_scalar(ss[:, c, :], ss[:, c, :], 2.0 ** NORM_SHIFT, 1e-24 * 2.0 ** NORM_SHIFT,
                                      ALU.mult, ALU.max).then_inc(s[clamp], 1)

                def normalise(c, k, n, inv, sin, norm):
                    dve.wait_ge(s[inv], n + 1)
                    wait_for(dve, s[sin], 2 * n)
                    dve.tensor_tensor(heads(qk_n[:, c, :]), heads(pa[k][:]), over(ss[:, c, :], DH), ALU.mult)\
                        .then_inc(s[norm], 1)

                def times_cos(c, i, n, norm, done, cos):
                    dve.wait_ge(s[norm], n + 1)
                    dve.wait_ge(s["rot_ready"], ROT_OPS * (i // GROUPS + 1))
                    wait_for(dve, s[done], n)
                    dve.tensor_tensor(heads(qk_r[:, c, :]), heads(qk_n[:, c, :]), per_head(rot[:, 2 * c, :]), ALU.mult)\
                        .then_inc(s[cos], 1)

                def new_layer(l):
                    for c in range(3):
                        at = slice(c * INNER, (c + 1) * INNER)
                        dve.wait_ge(s["w_hi_ready"], 3 * l + c + 1)
                        dve.tensor_tensor(w_lo[:, at], w_raw[:, at], w_hi[:, at].bitcast(F32), ALU.subtract)\
                            .then_inc(s["w_lo_ready"], 1)

                def turn_probs(n, lo, hi):
                    dve.wait_ge(s["probs_done"], n + 1)
                    wait_for(dve, s["pv_done"], n)
                    for b in range(lo, hi):
                        rows = slice(b * S, (b + 1) * S)
                        dve.transpose(pT[rows, :, rows], pr[rows, :]).then_inc(s["pT_done"], 1)

                def gated(g, k):
                    m = HBLK[k][1]
                    if k == 0:
                        dve.wait_ge(s["gelu_done"], g + 1)
                    dve.wait_ge(s["a_done"], 3 * g + k + 1)
                    dve.scalar_tensor_tensor(gt[0:m, k, :], pg[0:m, :], b1[0:m, 0, k:k + 1], gt[0:m, k, :],
                                             ALU.add, ALU.mult).then_inc(s["h_ready"], 1)

                def body(i):
                    for j in range(GT):
                        n, live = i * GT + j, Live(i, j)
                        u = 3 * j
                        if live.qkv:
                            sum_squares(0, n, "sq_q", "sum_q", "clamp_q", "inv_q")
                        if live.prev2 and j == 2:
                            gated(i - 2, 1)
                        if live.qkv:
                            normalise(0, u % 2, n, "inv_q", "sin_q", "norm_q")
                        if live.pv:
                            turn_probs(n - 2, 0, 1)
                        if live.prev2 and j == 0:
                            dve.wait_ge(s["frs_ready"], i - 1)
                            dve.wait_ge(s["ffn_loaded"], ((i - 2) // GROUPS + 1) * FFN_DMAS * 16)
                            dve.tensor_tensor(fn[:], fc[:], frs[:], ALU.mult).then_inc(s["fn_mul"], 1)
                            dve.wait_ge(s["fn_mul"], i - 1)
                            dve.tensor_scalar(fn[:], fn[:], ln_par[:, 0:1], ln_par[:, 1:2], ALU.mult, ALU.add)\
                                .then_inc(s["fn_ready"], 1)
                        if live.qkv:
                            sum_squares(1, n, "sq_k", "sum_k", "clamp_k", "inv_k")
                        if live.pv:
                            turn_probs(n - 2, 1, 2)
                        if live.qkv:
                            normalise(1, (u + 1) % 2, n, "inv_k", "sin_k", "norm_k")
                        if live.pv:
                            turn_probs(n - 2, 2, TILE_B)
                        if live.prev2 and j == 2:
                            gated(i - 2, 2)
                        if live.prev and j == 3:
                            dve.wait_ge(s["wo_done"], i)
                            r = res[:, bass.ds((i - 1) % GROUPS * GTOK, GTOK)]
                            dve.tensor_tensor(r, pg[:], r, ALU.add).then_inc(s["res_attn"], 1)
                        if live.qkv:
                            times_cos(0, i, n, "norm_q", "tq_done", "cos_q")
                        if live.score:
                            dve.wait_ge(s["scores_done"], n)
                            dve.tensor_reduce(top[:], keys(ps[:]), AX.X, ALU.max).then_inc(s["top_done"], 1)
                            dve.wait_ge(s["top_done"], n)
                            wait_for(dve, s["exp_done"], n - 1)
                            dve.tensor_tensor(keys(sm[:]), keys(ps[:]), over(top[:], S), ALU.subtract)\
                                .then_inc(s["sub_done"], 1)
                        if live.qkv:
                            times_cos(1, i, n, "norm_k", "tk_done", "cos_k")
                        if live.prev2 and j == 1:
                            gated(i - 2, 0)
                        if live.score:
                            dve.wait_ge(s["exp_done"], n)
                            dve.reduce_sum(den[:], keys(pr[:]), AX.X).then_inc(s["den_done"], 1)
                            dve.wait_ge(s["den_done"], n)
                            dve.reciprocal(rden[:], den[:]).then_inc(s["rden_done"], 1)
                        if live.prev2 and j == 2:
                            dve.wait_ge(s["w2_done"], i - 1)
                            r = res[:, bass.ds((i - 2) % GROUPS * GTOK, GTOK)]
                            dve.scalar_tensor_tensor(r, pg[:], ln_par[:, 2:3], r, ALU.add, ALU.add)\
                                .then_inc(s["res_ready"], 1)

                dve.memset(eps_c[:], LN_EPS).then_inc(s["zeroed"], 1)
                dve.memset(norm_c[:], 0.5 * NORM_SHIFT * float(np.log(2.0))).then_inc(s["zeroed"], 1)
                dve.memset(gt[:], 0.0).then_inc(s["zeroed"], 1)
                dve.wait_ge(s["const_loaded"], 5 * 16)
                dve.tensor_copy(ident_b[:], ident[:]).then_inc(s["mask_ready"], 1)
                dve.tensor_copy(mask_b[:], mask_f[:]).then_inc(s["mask_ready"], 1)
                dve.memset(top[:], 0.0).then_inc(s["res_ready"], GROUPS)
                group_steps(dve, body, new_layer)

            @block.gpsimd
            def _(pool):
                def shift_lo(n, k):
                    at = bass.ds((n % TILES) * P, P)
                    rest = lambda dst, src: pool.tensor_tensor(dst, src, hi, ALU.subtract)
                    pool.wait_ge(s["xs_hi_ready"], 2 * n + 2)
                    hi = xs_hi[0:64, k, :].bitcast(F32)
                    rest(xs_lo[0:64, k, :], res[0:64, at]).then_inc(s["xs_ready"], 1)
                    pool.wait_ge(s["xs_ready"], 2 * n + 1)
                    hi = xs_hi[64:P, k, :].bitcast(F32).rearrange("p (b t) -> p b t", t=S)[:, :, 1:S]
                    late(rest, xs_lo[64:P, k, :], res[64:P, at]).then_inc(s["xs_ready"], 1)
                    pool.wait_ge(s["xs_ready"], 2 * n + 2)

                def times_sin(c, n, norm, sin, rot_done):
                    pool.wait_ge(s[norm], n + 1)
                    wait_for(pool, s[rot_done], n)
                    src, dst = halves(qk_n[:, c, :]), halves(qk_t[:, c, :])
                    table = rot[:, 2 * c + 1, :].rearrange("p (f e) -> p f e", f=2)
                    for f in range(2):
                        pool.tensor_tensor(dst[:, :, f, :], src[:, :, 1 - f, :],
                                           table[:, f, :].unsqueeze(1).to_broadcast([P, HEADS, DH // 2]), ALU.mult)\
                            .then_inc(s[sin], 1)

                def rotate(c, n, cos, sin, rot_done):
                    pool.wait_ge(s[sin], 2 * n + 2)
                    pool.wait_ge(s[cos], n + 1)
                    pool.tensor_tensor(qk_r[:, c, :], qk_r[:, c, :], qk_t[:, c, :], ALU.add).then_inc(s[rot_done], 1)

                def new_layer(l):
                    pool.wait_ge(s["qk_scale_loaded"], 32 * (l + 1))
                    if not isinstance(l, int):
                        pool.wait_ge(s["cos_k"], l * TILES)
                        pool.wait_ge(s["sin_k"], 2 * l * TILES)
                    for c in range(2):
                        sc = qk_scale[:, c, :]
                        pool.tensor_tensor(rot[:, 2 * c, :], rot_const[:, 2 * c, :], sc, ALU.mult)\
                            .then_inc(s["rot_ready"], 1)
                        for f in range(2):
                            to, frm = slice(f * DH // 2, (f + 1) * DH // 2), slice((1 - f) * DH // 2, (2 - f) * DH // 2)
                            pool.tensor_tensor(rot[:, 2 * c + 1, to], rot_const[:, 2 * c + 1, to], sc[:, frm], ALU.mult)\
                                .then_inc(s["rot_ready"], 1)

                def body(i):
                    for j in range(GT):
                        n, live = i * GT + j, Live(i, j)
                        if live.qkv and j == 0:
                            pool.wait_ge(s["rot_ready"], ROT_OPS * (i // GROUPS + 1))
                        if live.qkv:
                            times_sin(0, n, "norm_q", "sin_q", "rot_q")
                            times_sin(1, n, "norm_k", "sin_k", "rot_k")
                            if not isinstance(n, int) or n + 1 < NT:
                                shift_lo(n + 1, (j + 1) % 2)
                            rotate(0, n, "cos_q", "sin_q", "rot_q")
                            rotate(1, n, "cos_k", "sin_k", "rot_k")
                        if live.score:
                            pool.wait_ge(s["rden_done"], n)
                            pool.tensor_tensor(keys(pr[:]), keys(pr[:]), over(rden[:], S), ALU.mult)\
                                .then_inc(s["probs_done"], 1)

                pool.memset(kT[:], 0.0).then_inc(s["zeroed"], 1)
                pool.memset(pT[:], 0.0).then_inc(s["zeroed"], 1)
                pool.memset(xs_hi[:].bitcast(F32), 0.0).then_inc(s["zeroed"], 1)
                pool.memset(xs_lo[:].bitcast(F32), 0.0).then_inc(s["zeroed"], 1)
                pool.memset(fs[:], 0.0).then_inc(s["zeroed"], 1)
                pool.wait_ge(s["zeroed"], 8)
                pool.wait_ge(s["const_loaded"], 5 * 16)
                shift_lo(0, 0)
                group_steps(pool, body, new_layer)



def add_input(nc, d, res):
    with ExitStack() as ctx:
        def sb(name, shape):
            return ctx.enter_context(nc.sbuf_tensor(name, shape, F32))

        def sem(name):
            return ctx.enter_context(nc.semaphore(name))

        ident = sb("o_ident", [P, P])
        x_in = sb("o_x", [P, GROUPS, GT, DM])
        out = sb("o_out", [P, GROUPS, GT, DM])
        pt = [ctx.enter_context(nc.psum_tensor(f"o_pt{k}", [P, GTOK], F32)) for k in range(2)]
        ident_loaded, turned, added, stored = sem("o_loaded"), sem("o_turned"), sem("o_added"), sem("o_stored")
        x_loaded = [sem(f"o_x_loaded{g}") for g in range(GROUPS)]
        view = lambda ap: ap.rearrange("b t m -> (b t) m").rearrange("(g k p) m -> g p k m", k=GT, p=P)
        x_v, out_v = view(d["x"]), view(d["out"])

        with nc.Block() as block:
            @block.sync
            def _(sp):
                sp.dma_start(ident[:], d["ident"]).then_inc(ident_loaded, 16)
                for g in range(GROUPS):
                    sp.dma_start(x_in[:, g], x_v[g]).then_inc(x_loaded[g], 16)
                for g in range(GROUPS):
                    sp.wait_ge(added, g + 1)
                    sp.dma_start(out_v[g], out[:, g]).then_inc(stored, 16)
                sp.wait_ge(stored, 16 * GROUPS)

            @block.tensor
            def _(pe):
                pe.wait_ge(ident_loaded, 16)
                for g in range(GROUPS):
                    wait_for(pe, added, g - 1)
                    for c in range(GT):
                        at = g * GTOK + c * P
                        last = pe.transpose(pt[g % 2][:, c * P:(c + 1) * P], res[:, at:at + P], ident[:])
                    last.then_inc(turned, 1)

            @block.vector
            def _(dve):
                for g in range(GROUPS):
                    dve.wait_ge(turned, g + 1)
                    dve.wait_ge(x_loaded[g], 16)
                    dve.tensor_tensor(out[:, g].rearrange("p c m -> p (c m)"), pt[g % 2][:],
                                      x_in[:, g].rearrange("p c m -> p (c m)"), ALU.add).then_inc(added, 1)


def build(nc, d):
    with ExitStack() as ctx:
        ctx.enter_context(nc.allow_non_contiguous_dma(reason="small parameters laid out as columns"))
        res = ctx.enter_context(nc.sbuf_tensor("res", [DM, TOKENS], F32))
        cond_block(nc, d, res)
        stack(nc, d, res)
        add_input(nc, d, res)


_INS = {
    "x": "x", "cond_2048": "cond", "L0_cond_W_in": "W_in", "L0_cond_W_conv": "W_conv", "L0_cond_b_conv": "b_conv",
    "L0_cond_ln_g": "ln_g", "L0_cond_ln_b": "ln_b", "L0_cond_W_xproj": "W_xproj", "L0_cond_W_dt": "W_dt",
    "L0_cond_b_dt": "b_dt", "L0_cond_A_log": "A_log", "L0_cond_D": "D", "L0_cond_W_out": "W_out",
    "L0_ffn_Wqkv": "Wqkv", "L0_ffn_q_scale": "q_scale", "L0_ffn_k_scale": "k_scale", "L0_ffn_Wo": "Wo",
    "L0_ffn_ln_g": "ffn_ln_g", "L0_ffn_ln_b": "ffn_ln_b", "L0_ffn_W1": "W1", "L0_ffn_b1": "b1", "L0_ffn_W2": "W2",
    "L0_ffn_b2": "b2",
}


def _shape_constants():
    f = np.float32
    eye = np.eye(P, dtype=f)
    mean = np.full((P, P), 1.0 / DM, f)
    q, k = np.arange(P)[:, None] % S, np.arange(HEADS * S)[None, :] % S
    mask = np.where(k <= q, f(0), f(NEG))
    half = np.arange(0, DH, 2, dtype=f)
    inv_freq = f(1) / np.power(f(10000), half / f(DH))
    t = np.arange(S, dtype=f)
    freqs = t[:, None] * inv_freq[None, :]
    scale = ((half + f(0.4 * DH)) / f(1.4 * DH))[None, :] ** ((t - f(S // 2)) / f(S // 2))[:, None]
    cos, sin = np.cos(freqs), np.sin(freqs)
    row = lambda a, b: np.concatenate([a, b], -1)
    rot = np.concatenate([row(cos * scale, cos * scale), row(-sin * scale, sin * scale),
                          row(cos / scale, cos / scale), row(-sin / scale, sin / scale)], -1)
    rot = np.tile(rot, (P // S, 1))
    return {"ident": eye, "center": eye - mean, "mean": mean, "mask": mask.astype(f), "rot": rot.astype(f)}


def kernel(**inputs):
    import concourse.bacc as bacc
    from concourse.bass_utils import run_bass_kernel_spmd

    nc = bacc.Bacc("TRN2", target_bir_lowering=False, num_devices=1)
    arrays = {short: np.ascontiguousarray(inputs[name]) for name, short in _INS.items()}
    arrays.update(_shape_constants())
    d, maps = {}, {}
    for name, a in arrays.items():
        maps[f"in_{name}"] = a
        d[name] = nc.dram_tensor(f"in_{name}", a.shape, mybir.dt.from_np(a.dtype), kind="ExternalInput").ap()
    d["out"] = nc.dram_tensor("out_0", (B, S, DM), F32, kind="ExternalOutput").ap()
    build(nc, d)
    r = run_bass_kernel_spmd(nc, [maps], core_ids=[0])
    return r.results[0]["out_0"]
```
